# Optimizing a Trainium2 kernel written in Bass

```python
import numpy as np
import jax
import jax.numpy as jnp

def _softmax(x, axis=-1):
    return jax.nn.softmax(x, axis=axis)

def _gelu(x):
    return jax.nn.gelu(x, approximate=True)

def _silu(x):
    return jax.nn.silu(x)

def _sigmoid(x):
    return jax.nn.sigmoid(x)

def _layernorm(x, axis=-1, eps=1e-05):
    m = jnp.mean(x, axis=axis, keepdims=True)
    v = jnp.var(x, axis=axis, keepdims=True)
    return (x - m) / jnp.sqrt(v + eps)

def _scatter_add(tgt, idx, src, axis=0):
    return tgt.at[idx].add(src)

def _segment_sum(src, seg, n):
    return jax.ops.segment_sum(src, seg, n)
kernel_name = 'mk_prb_d1_jaxref_r4_f7e078'

def setup_inputs(seed: int=0):
    np.random.seed(seed)
    _w = jnp.asarray

    def _L0_attn_setup():
        import jax, jax.numpy as jnp
        import numpy as np
        import math
        D = 256
        H = 16
        DH = D // H
        K = 64
        W = 128
        IDX = 64
        B, S = (1, 512)
        key = jax.random.key(seed)
        ks = jax.random.split(key, 16)
        sD = 1.0 / math.sqrt(D)
        x = jax.random.normal(ks[0], (B, S, D), jnp.float32)
        mk = lambda i, shp: jax.random.normal(ks[i], shp, jnp.float32) * sD
        return {'x': x, 'wq': mk(1, (D, D)), 'bq': mk(2, (D,)), 'wk': mk(3, (D, D)), 'bk': mk(4, (D,)), 'wv': mk(5, (D, D)), 'bv': mk(6, (D,)), 'wo': mk(7, (D, D)), 'bo': mk(8, (D,)), 'wqi': mk(9, (IDX, D)), 'bqi': mk(10, (IDX,)), 'wki': mk(11, (IDX, D)), 'bki': mk(12, (IDX,))}
    _L0_attn_in = _L0_attn_setup()

    def _L0_ffn_setup():
        import jax, jax.numpy as jnp
        import numpy as np
        D_MODEL = 256
        M = 64
        INNER = 16
        key = jax.random.key(seed)
        ks = jax.random.split(key, 9)

        def init(k, shape, fan_in):
            bound = 1.0 / np.sqrt(fan_in)
            return jax.random.uniform(k, shape, jnp.float32, -bound, bound)
        x = jax.random.normal(ks[0], (16, 1024, D_MODEL), dtype=jnp.float32)
        Win = init(ks[1], (D_MODEL, M), D_MODEL)
        bin_ = init(ks[2], (M,), D_MODEL)
        W1 = init(ks[3], (M, INNER), 1)
        b1 = init(ks[4], (M, INNER), 1)
        W2 = init(ks[5], (M, INNER), INNER)
        b2 = init(ks[6], (M,), INNER)
        Wout = init(ks[7], (M, D_MODEL), M)
        bout = init(ks[8], (D_MODEL,), M)
        return {'x': x, 'Win': Win, 'bin_': bin_, 'W1': W1, 'b1': b1, 'W2': W2, 'b2': b2, 'Wout': Wout, 'bout': bout}
    _L0_ffn_in = _L0_ffn_setup()
    _d = {'L0_attn_x': _L0_attn_in['x'], 'L0_attn_wq': _L0_attn_in['wq'], 'L0_attn_bq': _L0_attn_in['bq'], 'L0_attn_wk': _L0_attn_in['wk'], 'L0_attn_bk': _L0_attn_in['bk'], 'L0_attn_wv': _L0_attn_in['wv'], 'L0_attn_bv': _L0_attn_in['bv'], 'L0_attn_wo': _L0_attn_in['wo'], 'L0_attn_bo': _L0_attn_in['bo'], 'L0_attn_wqi': _L0_attn_in['wqi'], 'L0_attn_bqi': _L0_attn_in['bqi'], 'L0_attn_wki': _L0_attn_in['wki'], 'L0_attn_bki': _L0_attn_in['bki'], 'L0_ffn_Win': _L0_ffn_in['Win'], 'L0_ffn_bin_': _L0_ffn_in['bin_'], 'L0_ffn_W1': _L0_ffn_in['W1'], 'L0_ffn_b1': _L0_ffn_in['b1'], 'L0_ffn_W2': _L0_ffn_in['W2'], 'L0_ffn_b2': _L0_ffn_in['b2'], 'L0_ffn_Wout': _L0_ffn_in['Wout'], 'L0_ffn_bout': _L0_ffn_in['bout']}
    _x0 = _d['L0_attn_x']
    _d['L0_attn_x'] = jax.random.normal(jax.random.fold_in(jax.random.key(seed), 1), (4, 2048, 256), dtype=_x0.dtype)
    del _x0
    return _d

def reference(L0_attn_x, L0_attn_wq, L0_attn_bq, L0_attn_wk, L0_attn_bk, L0_attn_wv, L0_attn_bv, L0_attn_wo, L0_attn_bo, L0_attn_wqi, L0_attn_bqi, L0_attn_wki, L0_attn_bki, L0_ffn_Win, L0_ffn_bin_, L0_ffn_W1, L0_ffn_b1, L0_ffn_W2, L0_ffn_b2, L0_ffn_Wout, L0_ffn_bout):

    def _L0_attn_ref(x, wq, bq, wk, bk, wv, bv, wo, bo, wqi, bqi, wki, bki):
        import jax, jax.numpy as jnp
        import numpy as np
        import math
        D = 256
        H = 16
        DH = D // H
        K = 64
        W = 128
        IDX = 64
        B, S = (1, 512)
        Bx, Sx, _ = x.shape
        scale = 1.0 / math.sqrt(DH)

        def proj(w, b):
            return (x @ w.T + b).reshape(Bx, Sx, H, DH).transpose(0, 2, 1, 3)
        q, k, v = (proj(wq, bq), proj(wk, bk), proj(wv, bv))
        A = Sx - W
        k_work, v_work = (k[:, :, A:], v[:, :, A:])
        k_assoc, v_assoc = (k[:, :, :A], v[:, :, :A])
        scores_work = jnp.einsum('bhsd,bhwd->bhsw', q, k_work) * scale
        q_idx = x @ wqi.T + bqi
        k_idx = x[:, :A] @ wki.T + bki
        idx_scores = jax.nn.relu(jnp.einsum('bse,bae->bsa', q_idx, k_idx))
        kk = min(K, A)
        _, top_idx = jax.lax.top_k(idx_scores, kk)
        gather = jax.vmap(lambda kv, ix: kv[:, ix])
        k_g = gather(k_assoc, top_idx)
        v_g = gather(v_assoc, top_idx)
        scores_assoc = jnp.einsum('bhsd,bhskd->bhsk', q, k_g) * scale
        wmask = jnp.arange(W)[None, :] - jnp.arange(Sx)[:, None] >= 1 + A
        scores_work = jnp.where(wmask[None, None], -jnp.inf, scores_work)
        weights = jax.nn.softmax(jnp.concatenate([scores_assoc, scores_work], axis=-1), axis=-1)
        out = jnp.einsum('bhsk,bhskd->bhsd', weights[..., :kk], v_g) + jnp.einsum('bhsw,bhwd->bhsd', weights[..., kk:], v_work)
        out = out.transpose(0, 2, 1, 3).reshape(Bx, Sx, D)
        return out @ wo.T + bo

    def _L0_ffn_ref(x, Win, bin_, W1, b1, W2, b2, Wout, bout):
        import jax, jax.numpy as jnp
        import numpy as np
        D_MODEL = 256
        M = 64
        INNER = 16
        s = jnp.einsum('btd,dm->btm', x, Win) + bin_
        h = jax.nn.relu(s[..., None] * W1 + b1)
        g = jnp.einsum('btmh,mh->btm', h, W2) + b2
        out = jnp.einsum('btm,md->btd', g, Wout) + bout
        return out
    x = L0_attn_x
    xn = _layernorm(x, axis=-1)
    x = x + _L0_attn_ref(xn, L0_attn_wq, L0_attn_bq, L0_attn_wk, L0_attn_bk, L0_attn_wv, L0_attn_bv, L0_attn_wo, L0_attn_bo, L0_attn_wqi, L0_attn_bqi, L0_attn_wki, L0_attn_bki) + _L0_ffn_ref(xn, L0_ffn_Win, L0_ffn_bin_, L0_ffn_W1, L0_ffn_b1, L0_ffn_W2, L0_ffn_b2, L0_ffn_Wout, L0_ffn_bout)
    return x

_drawn_inputs = setup_inputs


def setup_inputs(seed=0):
    import zlib

    import numpy as np

    out = dict(_drawn_inputs(seed))
    spreads = {}
    factors = {'L0_attn_bq': 6.749,
     'L0_attn_bk': 64.0,
     'L0_attn_bqi': 2.837,
     'L0_ffn_bin_': 8.0,
     'L0_attn_bki': 8.0}
    for name, (base, spread) in spreads.items():
        noise = np.random.default_rng([zlib.crc32(name.encode()), seed]).standard_normal(out[name].shape)
        drawn = base * np.exp(spread * noise) if base else spread * noise
        out[name] = jnp.asarray(drawn.astype(out[name].dtype))
    for name, factor in factors.items():
        out[name] = (out[name] * factor).astype(out[name].dtype)
    return out
```

```python
import concourse.bass as bass
from concourse import mybir
from contextlib import ExitStack

BATCH, SEQ, DIM = 4, 2048, 256
HEADS, HEAD_DIM = 16, 16
TOPK, WINDOW, INDEX_DIM = 64, 128, 64
FFN_M, FFN_INNER = 64, 16
EPS = 1e-5
P = 128

TOKENS = BATCH * SEQ
CHUNK = 512
CHUNKS = TOKENS // CHUNK
TILES = CHUNK // P
CC = DIM // P
ASSOC = SEQ - WINDOW
ASSOC_TILES = ASSOC // P
KEY_TILES = SEQ // P
QUADS = HEADS // 4
SCALE = 0.25
V_COLS = HEAD_DIM + 1

PAIRS = ((0, 0), (0, 1), (1, 0), (1, 1), (0, 2), (2, 0))
STACK = len(PAIRS) * HEAD_DIM
SHIFT_ROWS = 3
ROWS = STACK + SHIFT_ROWS
EXCLUDED = -1e30

SPREAD_LIMIT = 75.0
BF16_ONES = 1.0019378662109375

STEPS = QUADS * KEY_TILES
WINDOW_STEPS = STEPS // TILES


def misc_jobs():
    at = {}
    for i in range(TILES):
        at[i + (i > 1)] = ("norm", i)
    at[7], at[9] = ("turn", 0), ("turn", 1)
    at[12], at[14] = ("proj", 0), ("proj", 1)
    for t in range(TILES):
        for i, r in enumerate((2, 5, 8, 11)):
            at[WINDOW_STEPS * t + r] = ("index", (t, i))
        for i, r in enumerate((6, 13)):
            at[WINDOW_STEPS * t + r] = ("mask", (t, i))
    free = [s for s in range(WINDOW_STEPS - 1, 3 * WINDOW_STEPS) if s not in at]
    for i in range(TILES * QUADS):
        at[free[i]] = ("window", (i // QUADS, i % QUADS))
    at[3 * WINDOW_STEPS + 3] = ("shift", 0)
    return {s: (n, *at[s]) for n, s in enumerate(sorted(at))}


JOBS = misc_jobs()
NJOBS = len(JOBS)
INDEX_LEAD, TOPK_LEAD, MASK_LEAD = 6, 5, 4
INDEX_PIECES = 4
PIECE = ASSOC // INDEX_PIECES
MASK_SPLIT = (0, 8, ASSOC_TILES)
PRO_JOBS = INDEX_LEAD * INDEX_PIECES + MASK_LEAD * 2 + TILES * QUADS + 1


def stand(engine, passed):
    engine.sem_inc(passed, 1)


def job_position(kind, arg):
    return [n for n, k, a in JOBS.values() if (k, a) == (kind, arg)][0]


def build(nc, x, wq, bq, wk, bk, wv, bv, wo, bo, wqi, bqi, wki, bki, Win, bin_, W1, b1, W2, b2, Wout, bout, out):
    f32, bf16, f8, i32 = mybir.dt.float32, mybir.dt.bfloat16, mybir.dt.float8e4, mybir.dt.int32
    ALU, ACT, AX = mybir.AluOpType, mybir.ActivationFunctionType, mybir.AxisListType

    x_rows = x.rearrange("b s d -> (b s) d")
    out_rows = out.rearrange("b s d -> (b s) d")
    q_parts = nc.dram_tensor("q_parts", (3, DIM, TOKENS), bf16, kind="Internal").ap()
    k_parts = nc.dram_tensor("k_parts", (3, DIM, TOKENS), bf16, kind="Internal").ap()
    values = nc.dram_tensor("values", (TOKENS, HEADS * V_COLS), f32, kind="Internal").ap()
    index_qk = nc.dram_tensor("index_qk", (2 * INDEX_DIM, TOKENS), f32, kind="Internal").ap()
    residual = nc.dram_tensor("residual", (TOKENS, DIM), f32, kind="Internal").ap()

    with ExitStack() as whole:
        ident = whole.enter_context(nc.sbuf_tensor("ident", [P, P], f32))
        ident_b = whole.enter_context(nc.sbuf_tensor("ident_b", [P, P], bf16))
        exclude_diag = whole.enter_context(nc.sbuf_tensor("exclude_diag", [P, P], bf16))
        woT = whole.enter_context(nc.sbuf_tensor("woT", [P, CC, DIM], f32))
        flag = whole.enter_context(nc.sbuf_tensor("flag", [1, 1], i32))
        phase_one(nc, x_rows, wq, bq, wk, bk, wv, bv, wo, bo, wqi, bqi, wki, bki, Win, bin_, W1, b1, W2, b2,
                  Wout, bout, q_parts, k_parts, values, index_qk, residual,
                  ident, ident_b, exclude_diag, woT, flag)
        phase_two(nc, q_parts, k_parts, values, index_qk, residual, out_rows,
                  ident, ident_b, exclude_diag, woT, flag)


def phase_one(nc, x_rows, wq, bq, wk, bk, wv, bv, wo, bo, wqi, bqi, wki, bki, Win, bin_, W1, b1, W2, b2,
              Wout, bout, q_parts, k_parts, values, index_qk, residual,
              ident, ident_b, exclude_diag, woT, flag):
    f32, bf16, i32 = mybir.dt.float32, mybir.dt.bfloat16, mybir.dt.int32
    ALU, ACT, AX = mybir.AluOpType, mybir.ActivationFunctionType, mybir.AxisListType
    PAIRS_J = FFN_INNER // 2

    OUTS = [("xT0", "act"), ("xT1", "dve"), ("s", "act"), ("q0", "dve"), ("q1", "dve"), ("k0", "dve"),
            ("k1", "dve"), ("v0", "dve"), ("v1", "dve"), ("index", "act"), ("norms", "dve"), ("g", "dve"),
            ("ffn0", "dve"), ("ffn1", "dve")]
    NAMES = [n for n, _ in OUTS]
    ACT_FREES = ["xT0", "s", "index"]
    DVE_FREES = ["xT1", "q0", "q1", "k0", "k1", "v0", "v1", "norms", "g", "ffn0", "ffn1"]

    with ExitStack() as ctx:
        def sb(name, shape, dt=f32):
            return ctx.enter_context(nc.sbuf_tensor(name, shape, dt))

        def sem(name):
            return ctx.enter_context(nc.semaphore(name))

        w_nat = sb("w_nat", [P, 4, CC, DIM])
        wi_nat = sb("wi_nat", [P, DIM])
        wT = sb("wT", [P, 3, CC, DIM])
        wiT = sb("wiT", [P, CC, P])
        win = sb("win", [P, CC, 2, FFN_M])
        wout = sb("wout", [P, DIM])
        bq_raw = sb("bq_raw", [P, CC])
        bq_c = sb("bq_c", [P, CC])
        bk_c = sb("bk_c", [P, CC])
        bi_c = sb("bi_c", [P, 1])
        bin_c = sb("bin_c", [P, 1])
        b2_c = sb("b2_c", [P, 1])
        w1_c = sb("w1_c", [P, PAIRS_J])
        b1_c = sb("b1_c", [P, PAIRS_J])
        w2_c = sb("w2_c", [P, PAIRS_J])
        rows = sb("rows", [1, 3, DIM])
        ones = sb("ones", [1, P])
        bv_b = sb("bv_b", [P, DIM])
        bo_b = sb("bo_b", [P, DIM])
        ident2 = sb("ident2", [P, FFN_M])
        w2_diag = sb("w2_diag", [P, PAIRS_J, FFN_M])
        head_sum = sb("head_sum", [P, 8])
        head_sel = sb("head_sel", [P, 32], bf16)

        x_in = sb("x_in", [P, 2, TILES, DIM])
        stats = sb("stats", [P, TILES, 6])
        mean_var = sb("mean_var", [P, TILES, 2])
        var_eps = sb("var_eps", [P, TILES])
        std = sb("std", [P, TILES])
        rstd = sb("rstd", [P, TILES])
        xn = sb("xn", [P, TILES, DIM])
        xnT = sb("xnT", [P, CC, CHUNK])
        parts = sb("parts", [P, 2, CC, 3, CHUNK], bf16)
        rest = sb("rest", [P, 2, CC, CHUNK])
        squares = sb("squares", [P, 2, CC, CHUNK], bf16)
        v_out = sb("v_out", [P, TILES, HEADS, V_COLS])
        i_out = sb("i_out", [P, CHUNK])
        sT = sb("sT", [P, CHUNK])
        hidden = sb("hidden", [P, PAIRS_J, CHUNK])
        gT = sb("gT", [P, CHUNK])
        res = sb("res", [P, TILES, DIM])
        norm_now = sb("norm_now", [P, 1])
        norm_max = sb("norm_max", [P, 1])
        norm_row = sb("norm_row", [1, P])
        bound = sb("bound", [1, P // 2])
        bound_max = sb("bound_max", [1, 1])
        over = sb("over", [1, 1])
        bank = [ctx.enter_context(nc.psum_tensor(f"bank{i}", [P, CHUNK], f32)) for i in range(8)]

        w_loaded, ffn_loaded = sem("w_loaded"), sem("ffn_loaded")
        x_loaded = [sem(f"x_loaded{u}") for u in range(2)]
        ident_ready, setup_dve, setup_pe = sem("ident_ready"), sem("setup_dve"), sem("setup_pe")
        norm_step, std_ready, xn_ready = sem("norm_step"), sem("std_ready"), sem("xn_ready")
        pe_out, act_freed, dve_freed = sem("pe_out"), sem("act_freed"), sem("dve_freed")
        first_part, hidden_ready, max_kept = sem("first_part"), sem("hidden_ready"), sem("max_kept")
        second_part, third_part, res_ready = sem("second_part"), sem("third_part"), sem("res_ready")
        parts_stored, v_stored, i_stored, res_stored = (sem("parts_stored"), sem("v_stored"), sem("i_stored"),
                                                        sem("res_stored"))
        final, passed = sem("final"), sem("passed")
        TABLES, FFN_TABLES = 20, 6
        block = ctx.enter_context(nc.Block())

        def out_bank(name):
            return bank[NAMES.index(name) % 8]

        def filled(name, k):
            return k * len(OUTS) + NAMES.index(name) + 1

        def act_count(name, k):
            return len(ACT_FREES) * (k + 1) + ACT_FREES.index(name) + 1

        def dve_count(name, k):
            return len(DVE_FREES) * (k + 1) + DVE_FREES.index(name) + 1

        @block.sync
        def _(sp):
            for i, w in enumerate((wq, wk, wv, wo)):
                sp.dma_start(w_nat[:, i], w.rearrange("(t p) c -> p t c", p=P)).then_inc(w_loaded, 16)
            sp.dma_start(wi_nat[0:INDEX_DIM], wqi).then_inc(w_loaded, 16)
            sp.dma_start(wi_nat[INDEX_DIM:P], wki).then_inc(w_loaded, 16)
            sp.dma_start(x_in[:, 0], x_rows[0:CHUNK].rearrange("(t p) d -> p t d", p=P)).then_inc(x_loaded[0], 16)
            for i, b in enumerate((bv, bo, bout)):
                sp.dma_start(rows[:, i], b.rearrange("(o n) -> o n", o=1)).then_inc(w_loaded, 16)
            sp.dma_start(bi_c[0:INDEX_DIM], bqi.rearrange("(p o) -> p o", o=1)).then_inc(w_loaded, 16)
            sp.dma_start(bi_c[INDEX_DIM:P], bki.rearrange("(p o) -> p o", o=1)).then_inc(w_loaded, 16)
            sp.wait_ge(setup_dve, 1)
            sp.dma_start(b2_c[0:FFN_M], b2.rearrange("(p o) -> p o", o=1)).then_inc(w_loaded, 16)
            sp.dma_start(x_in[:, 1], x_rows[CHUNK:2 * CHUNK].rearrange("(t p) d -> p t d", p=P)).then_inc(x_loaded[1], 16)
            with sp.Fori(0, CHUNKS // 2) as m:
                for u in range(2):
                    k = 2 * m + u
                    rows_k = bass.ds(k * CHUNK, CHUNK)
                    sp.wait_ge(res_ready, k + 1)
                    sp.wait_ge(xn_ready, k + 1)
                    after = (k + 2) % CHUNKS
                    sp.dma_start(x_in[:, u], x_rows[bass.ds(after * CHUNK, CHUNK)].rearrange("(t p) d -> p t d", p=P))\
                        .then_inc(x_loaded[u], 16)
                    for i, dst in enumerate((q_parts, k_parts)):
                        for c in range(CC):
                            sp.wait_ge(third_part, 4 * k + 2 * i + c + 1)
                            sp.dma_start(dst[:, c * P:(c + 1) * P, rows_k].rearrange("j d t -> d j t"),
                                         parts[:, i, c]).then_inc(parts_stored, 16)
                    sp.wait_ge(dve_freed, dve_count("v1", k))
                    sp.dma_start(values[rows_k].rearrange("(t p) c -> p t c", p=P),
                                 v_out[:, :, :, :].rearrange("p t h v -> p t (h v)")).then_inc(v_stored, 16)
                    sp.wait_ge(act_freed, act_count("index", k))
                    stand(sp, passed)
                    sp.dma_start(index_qk[:, rows_k], i_out[:, :]).then_inc(i_stored, 16)
                    sp.wait_ge(dve_freed, dve_count("ffn1", k))
                    sp.dma_start(residual[rows_k].rearrange("(t p) d -> p t d", p=P), res[:, :, :])\
                        .then_inc(res_stored, 16)
            sp.wait_ge(parts_stored, 64 * (CHUNKS + 1))
            sp.wait_ge(v_stored, 16 * (CHUNKS + 1))
            sp.wait_ge(i_stored, 16 * (CHUNKS + 1))
            sp.wait_ge(res_stored, 16 * (CHUNKS + 1))
            for u in range(2):
                sp.wait_ge(x_loaded[u], 16 * (CHUNKS // 2 + 1))

        @block.gpsimd
        def _(pool):
            nc.gpsimd.memset(ident[:], 0.0).then_inc(ident_ready, 1)
            pool.wait_ge(ident_ready, 1)
            nc.gpsimd.affine_select(out=ident[:], in_=ident[:], compare_op=ALU.not_equal, fill=1.0, base=0,
                                    pattern=[[-1, P]], channel_multiplier=1).then_inc(ident_ready, 1)
            nc.gpsimd.memset(v_out[:], 1.0).then_inc(ident_ready, 1)
            pool.wait_ge(setup_dve, 2)
            with pool.Fori(0, CHUNKS // 2) as m:
                for u in range(2):
                    k = 2 * m + u
                    pool.wait_ge(x_loaded[u], 16 * (m + 1))
                    pool.wait_ge(res_stored, 16 * (k + 1))
                    nc.gpsimd.tensor_tensor(res[:, :, :], x_in[:, u],
                                            bo_b[:, :].unsqueeze(1).to_broadcast([P, TILES, DIM]), ALU.add)\
                        .then_inc(res_ready, 1)
                    for i in range(2):
                        for c in range(CC):
                            n = 4 * k + 2 * i + c
                            pool.wait_ge(dve_freed, dve_count(f"{'qk'[i]}{c}", k))
                            stand(pool, passed)
                            nc.gpsimd.tensor_copy(parts[:, i, c, 1], rest[:, i, c]).then_inc(second_part, 1)
                            pool.wait_ge(second_part, n + 1)
                            nc.gpsimd.tensor_tensor(parts[:, i, c, 2], rest[:, i, c], parts[:, i, c, 1],
                                                    ALU.subtract).then_inc(third_part, 1)

        @block.scalar
        def _(act):
            for i in range(2):
                act.dma_start(win[:, :, i], Win.rearrange("(t p) m -> p t m", p=P)).then_inc(w_loaded, 16)
                half = slice(i * FFN_M, (i + 1) * FFN_M)
                act.dma_start(wout[half], Wout).then_inc(w_loaded, 16)
                act.dma_start(bin_c[half], bin_.rearrange("(p o) -> p o", o=1)).then_inc(w_loaded, 16)
            act.dma_start(bq_raw[:, :], bq.rearrange("(t p) -> p t", p=P), allow_slow_non_contiguous=True).then_inc(w_loaded, 16)
            act.dma_start(bk_c[:, :], bk.rearrange("(t p) -> p t", p=P), allow_slow_non_contiguous=True).then_inc(w_loaded, 16)
            for i in range(2):
                half = slice(i * FFN_M, (i + 1) * FFN_M)
                js = slice(i * PAIRS_J, (i + 1) * PAIRS_J)
                act.dma_start(w1_c[half], W1[:, js]).then_inc(ffn_loaded, 16)
                act.dma_start(b1_c[half], b1[:, js]).then_inc(ffn_loaded, 16)
                act.dma_start(w2_c[half], W2[:, js]).then_inc(ffn_loaded, 16)
            act.sem_inc(act_freed, len(ACT_FREES))
            act.sem_inc(parts_stored, 64)
            act.sem_inc(i_stored, 16)
            act.wait_ge(setup_dve, 2)
            act.wait_ge(w_loaded, 16 * TABLES)
            act.wait_ge(ffn_loaded, 16 * FFN_TABLES)
            act.wait_ge(norm_step, 3)
            nc.scalar.activation(std[:, :], var_eps[:, :], ACT.Sqrt).then_inc(std_ready, 1)
            with act.Fori(0, CHUNKS // 2) as m:
                for u in range(2):
                    k = 2 * m + u
                    act.wait_ge(pe_out, filled("xT0", k))
                    nc.scalar.activation(xnT[:, 0], out_bank("xT0")[:, :], ACT.Identity).then_inc(act_freed, 1)
                    act.wait_ge(pe_out, filled("s", k))
                    nc.scalar.activation(sT[:, :], out_bank("s")[:, :], ACT.Identity, bias=bin_c[:, 0:1])\
                        .then_inc(act_freed, 1)
                    act.wait_ge(act_freed, act_count("s", k))
                    for j in range(PAIRS_J):
                        h = nc.scalar.activation(hidden[:, j], sT[:, :], ACT.Relu, bias=b1_c[:, j:j + 1],
                                                 scale=w1_c[:, j:j + 1])
                    h.then_inc(hidden_ready, 1)
                    for i, (name, b) in enumerate((("q", bq_c), ("k", bk_c))):
                        for c in range(CC):
                            act.wait_ge(pe_out, filled(f"{name}{c}", k))
                            if i == 0 and c == 0:
                                act.wait_ge(parts_stored, 64 * (k + 1))
                            src = out_bank(f"{name}{c}")
                            nc.scalar.activation(parts[:, i, c, 0], src[:, :], ACT.Identity, bias=b[:, c:c + 1])
                            if i == 0:
                                sq = nc.scalar.activation(squares[:, i, c], src[:, :], ACT.Square, bias=b[:, c:c + 1])
                            else:
                                sq = nc.scalar.activation(squares[:, i, c], src[:, :], ACT.Square)
                            sq.then_inc(first_part, 1)
                    act.wait_ge(pe_out, filled("index", k))
                    act.wait_ge(i_stored, 16 * (k + 1))
                    nc.scalar.activation(i_out[:, :], out_bank("index")[:, :], ACT.Identity, bias=bi_c[:, 0:1])\
                        .then_inc(act_freed, 1)
                    act.wait_ge(norm_step, 4 * (k + 1) + 3)
                    nc.scalar.activation(std[:, :], var_eps[:, :], ACT.Sqrt).then_inc(std_ready, 1)

        @block.vector
        def _(dve):
            chain = [0]

            def step(ins):
                chain[0] += 1
                ins.then_inc(final, 1)
                dve.wait_ge(final, chain[0])

            nc.vector.memset(b2_c[:], 0.0).then_inc(setup_dve, 1)
            nc.vector.memset(ones[:], 1.0)
            nc.vector.memset(norm_max[:], 0.0)
            step(nc.vector.memset(head_sel[:], 0.0))
            dve.wait_ge(ident_ready, 3)
            nc.vector.tensor_copy(ident_b[:], ident[:])
            nc.vector.tensor_scalar(exclude_diag[:], ident[:], EXCLUDED, None, ALU.mult)
            nc.vector.tensor_tensor(ident2[:], ident[:, 0:FFN_M], ident[:, FFN_M:P], ALU.add)
            step(nc.vector.reduce_sum(head_sum[:], ident[:, :].rearrange("p (h i) -> p h i", i=HEAD_DIM), AX.X))
            step(nc.vector.tensor_copy(head_sel[:, 0:8], head_sum[:]))
            dve.wait_ge(w_loaded, 16 * TABLES)
            dve.wait_ge(ffn_loaded, 16 * FFN_TABLES)
            for j in range(PAIRS_J):
                nc.vector.tensor_scalar(w2_diag[:, j], ident2[:], w2_c[:, j:j + 1], None, ALU.mult)
            nc.vector.tensor_scalar(bq_c[:], bq_raw[:], SCALE, None, ALU.mult)
            dve.wait_ge(setup_pe, 1)
            for i in range(4):
                dst = woT if i == 3 else wT[:, i]
                nc.vector.tensor_scalar(dst[:, :, :], bank[i][:, :].rearrange("p (c n) -> p c n", c=CC),
                                        SCALE if i == 0 else 1.0, None, ALU.mult)
            nc.vector.tensor_copy(wiT[:, :, :], bank[4][:, 0:DIM].rearrange("p (c n) -> p c n", c=CC))
            nc.vector.tensor_copy(bv_b[:], bank[5][:, 0:DIM])
            step(nc.vector.tensor_copy(bo_b[:], bank[6][:, 0:DIM]))
            dve.sem_inc(dve_freed, len(DVE_FREES))
            dve.sem_inc(v_stored, 16)
            dve.sem_inc(res_stored, 16)
            dve.sem_inc(setup_dve, 1)

            def normalise(k, u, loads):
                dve.wait_ge(x_loaded[u], 16 * loads)
                for t in range(TILES):
                    s = nc.vector.bn_stats(stats[:, t], x_in[:, u, t])
                s.then_inc(norm_step, 1)
                dve.wait_ge(norm_step, 4 * k + 1)
                stand(dve, passed)
                for t in range(TILES):
                    s = nc.vector.bn_aggr(mean_var[:, t], stats[:, t])
                s.then_inc(norm_step, 1)
                dve.wait_ge(norm_step, 4 * k + 2)
                nc.vector.tensor_scalar(var_eps[:, :], mean_var[:, :, 1], EPS, None, ALU.add).then_inc(norm_step, 1)
                dve.wait_ge(std_ready, k + 1)
                nc.vector.reciprocal(rstd[:, :], std[:, :]).then_inc(norm_step, 1)
                dve.wait_ge(norm_step, 4 * k + 4)
                for t in range(TILES):
                    s = nc.vector.tensor_scalar(xn[:, t], x_in[:, u, t], mean_var[:, t, 0:1], rstd[:, t:t + 1],
                                                ALU.subtract, ALU.mult)
                s.then_inc(xn_ready, 1)

            normalise(0, 0, 1)
            with dve.Fori(0, CHUNKS // 2) as m:
                for u in range(2):
                    k = 2 * m + u
                    dve.wait_ge(pe_out, filled("xT1", k))
                    nc.vector.tensor_copy(xnT[:, 1], out_bank("xT1")[:, :]).then_inc(dve_freed, 1)
                    for i, (name, b) in enumerate((("q", bq_c), ("k", bk_c))):
                        for c in range(CC):
                            n = 4 * k + 2 * i + c
                            dve.wait_ge(first_part, n + 1)
                            if i == 0 and c == 0:
                                dve.wait_ge(parts_stored, 64 * (k + 1))
                            nc.vector.scalar_tensor_tensor(rest[:, i, c], out_bank(f"{name}{c}")[:, :], b[:, c:c + 1],
                                                           parts[:, i, c, 0], ALU.add, ALU.subtract)\
                                .then_inc(dve_freed, 1)
                    for c in range(2):
                        dve.wait_ge(pe_out, filled(f"v{c}", k))
                        if c == 0:
                            dve.wait_ge(v_stored, 16 * (k + 1))
                        nc.vector.tensor_tensor(
                            v_out[:, 2 * c:2 * c + 2, :, 0:HEAD_DIM],
                            out_bank(f"v{c}")[:, :].rearrange("p (t h i) -> p t h i", t=2, h=HEADS),
                            bv_b[:, :].rearrange("p (h i) -> p h i", h=HEADS).unsqueeze(1)
                            .to_broadcast([P, 2, HEADS, HEAD_DIM]), ALU.add).then_inc(dve_freed, 1)
                    normalise(k + 1, 1 - u, m + u + 1)
                    dve.wait_ge(pe_out, filled("norms", k))
                    nc.vector.reduce_max(norm_now[:, :], out_bank("norms")[:, :], AX.X)\
                        .then_inc(dve_freed, 1)
                    dve.wait_ge(dve_freed, dve_count("norms", k))
                    nc.vector.tensor_tensor(norm_max[:, :], norm_max[:, :], norm_now[:, :], ALU.max).then_inc(max_kept, 1)
                    dve.wait_ge(pe_out, filled("g", k))
                    nc.vector.tensor_scalar(gT[:, :], out_bank("g")[:, :], b2_c[:, 0:1], None, ALU.add)\
                        .then_inc(dve_freed, 1)
                    for c in range(2):
                        dve.wait_ge(pe_out, filled(f"ffn{c}", k))
                        if c == 0:
                            dve.wait_ge(res_ready, k + 1)
                        part = res[:, 2 * c:2 * c + 2]
                        nc.vector.tensor_tensor(part, out_bank(f"ffn{c}")[:, :].rearrange("p (t d) -> p t d", t=2),
                                                part, ALU.add).then_inc(dve_freed, 1)
            dve.wait_ge(setup_pe, 2)
            step(nc.vector.tensor_copy(norm_row[:], bank[0][0:1, 0:P]))
            step(nc.vector.tensor_tensor(bound[:], norm_row[:, 0:P // 2], norm_row[:, P // 2:P], ALU.mult))
            step(nc.vector.reduce_max(bound_max[:], bound[:], AX.X))
            step(nc.vector.tensor_scalar(over[:], bound_max[:], (SPREAD_LIMIT / 2) ** 2, None, ALU.is_gt))
            step(nc.vector.tensor_copy(flag[:], over[:]))

        @block.tensor
        def _(pe):
            pe.wait_ge(ident_ready, 2)
            pe.wait_ge(w_loaded, 16 * TABLES)
            pe.wait_ge(final, 1)
            for i in range(4):
                for c in range(CC):
                    for o in range(CC):
                        nc.tensor.transpose(bank[i][:, c * DIM + o * P:c * DIM + (o + 1) * P],
                                            w_nat[:, i, o, c * P:(c + 1) * P], ident[:])
            for c in range(CC):
                nc.tensor.transpose(bank[4][:, c * P:(c + 1) * P], wi_nat[:, c * P:(c + 1) * P], ident[:])
            nc.tensor.matmul(bank[5][:, 0:DIM], ones[:, :], rows[:, 0], start=True, stop=True)
            nc.tensor.matmul(bank[6][:, 0:DIM], ones[:, :], rows[:, 1], start=True, stop=False)
            nc.tensor.matmul(bank[6][:, 0:DIM], ones[:, :], rows[:, 2], start=False, stop=True).then_inc(setup_pe, 1)
            pe.wait_ge(setup_dve, 2)

            def bank_free(name, k):
                i = NAMES.index(name)
                if i >= 8:
                    before, kb = NAMES[i - 8], k
                elif i + 8 < len(OUTS):
                    before, kb = NAMES[i + 8], k - 1
                else:
                    before, kb = name, k - 1
                if dict(OUTS)[before] == "act":
                    pe.wait_ge(act_freed, act_count(before, kb))
                else:
                    pe.wait_ge(dve_freed, dve_count(before, kb))

            with pe.Fori(0, CHUNKS // 2) as m:
                for u in range(2):
                    k = 2 * m + u
                    pe.wait_ge(xn_ready, k + 1)
                    for c in range(CC):
                        bank_free(f"xT{c}", k)
                        for t in range(TILES):
                            tr = nc.tensor.transpose(out_bank(f"xT{c}")[:, t * P:(t + 1) * P],
                                                     xn[:, t, c * P:(c + 1) * P], ident[:])
                        tr.then_inc(pe_out, 1)
                    pe.wait_ge(act_freed, act_count("xT0", k))
                    pe.wait_ge(dve_freed, dve_count("xT1", k))
                    bank_free("s", k)
                    for c in range(CC):
                        mm = nc.tensor.matmul(out_bank("s")[:, :], win[:, c].rearrange("p a m -> p (a m)"), xnT[:, c],
                                              start=c == 0, stop=c == CC - 1)
                    mm.then_inc(pe_out, 1)
                    for i, name in enumerate("qk"):
                        for o in range(CC):
                            bank_free(f"{name}{o}", k)
                            for c in range(CC):
                                mm = nc.tensor.matmul(out_bank(f"{name}{o}")[:, :], wT[:, i, c, o * P:(o + 1) * P],
                                                      xnT[:, c], start=c == 0, stop=c == CC - 1)
                            mm.then_inc(pe_out, 1)
                    for o in range(2):
                        bank_free(f"v{o}", k)
                        for j in range(2):
                            t = 2 * o + j
                            for c in range(CC):
                                mm = nc.tensor.matmul(out_bank(f"v{o}")[:, j * DIM:(j + 1) * DIM],
                                                      xnT[:, c, t * P:(t + 1) * P], wT[:, 2, c],
                                                      start=c == 0, stop=c == CC - 1)
                        mm.then_inc(pe_out, 1)
                    bank_free("index", k)
                    for c in range(CC):
                        mm = nc.tensor.matmul(out_bank("index")[:, :], wiT[:, c], xnT[:, c],
                                              start=c == 0, stop=c == CC - 1)
                    mm.then_inc(pe_out, 1)
                    bank_free("norms", k)
                    pe.wait_ge(first_part, 4 * k + 4)
                    for i in range(2):
                        for c in range(CC):
                            q = 32 * (2 * i + c)
                            mm = nc.tensor.matmul(out_bank("norms")[q:q + 32, :], head_sel[:, :], squares[:, i, c],
                                                  start=True, stop=True)
                    mm.then_inc(pe_out, 1)
                    bank_free("g", k)
                    pe.wait_ge(hidden_ready, k + 1)
                    for j in range(PAIRS_J):
                        q = FFN_M * (j % 2)
                        mm = nc.tensor.matmul(out_bank("g")[q:q + FFN_M, :], w2_diag[:, j], hidden[:, j],
                                              start=j < 2, stop=j >= PAIRS_J - 2)
                    mm.then_inc(pe_out, 1)
                    pe.wait_ge(dve_freed, dve_count("g", k))
                    for o in range(2):
                        bank_free(f"ffn{o}", k)
                        for j in range(2):
                            t = 2 * o + j
                            mm = nc.tensor.matmul(out_bank(f"ffn{o}")[:, j * DIM:(j + 1) * DIM],
                                                  gT[:, t * P:(t + 1) * P], wout[:, :], start=True, stop=True)
                        mm.then_inc(pe_out, 1)
            pe.wait_ge(max_kept, CHUNKS)
            nc.tensor.matmul(bank[0][0:1, 0:P], norm_max[:, 0:1], ident[:, :], start=True, stop=True)\
                .then_inc(setup_pe, 1)


def phase_two(nc, q_parts, k_parts, values, index_qk, residual, out_rows,
              ident, ident_b, exclude_diag, woT, flag):
    f32, bf16, f8 = mybir.dt.float32, mybir.dt.bfloat16, mybir.dt.float8e4
    ALU, ACT, AX = mybir.AluOpType, mybir.ActivationFunctionType, mybir.AxisListType

    with ExitStack() as ctx:
        def sb(name, shape, dt=f32):
            return ctx.enter_context(nc.sbuf_tensor(name, shape, dt))

        def sem(name):
            return ctx.enter_context(nc.semaphore(name))

        keys = sb("keys", [P, HEADS, SEQ], bf16)
        queries = [sb(f"queries{u}", [P, HEADS, CHUNK], bf16) for u in range(2)]
        v_sb = sb("v_sb", [P, QUADS, KEY_TILES, 4 * V_COLS])
        window_keys = sb("window_keys", [P, HEADS, WINDOW], bf16)
        masks = [sb(f"masks{u}", [P, ASSOC_TILES, CHUNK], f8) for u in range(2)]
        index_k = sb("index_k", [INDEX_DIM, ASSOC])
        index_q = [sb(f"index_q{p}", [INDEX_DIM, P]) for p in range(2)]
        index_scores = [sb(f"index_scores{p}", [P, ASSOC]) for p in range(2)]
        top8 = sb("top8", [P, 8])
        left_out = sb("left_out", [P, ASSOC], bf16)
        probs = [sb(f"probs{p}", [P, 4, CHUNK]) for p in range(2)]
        heads_out = sb("heads_out", [P, QUADS, CHUNK])
        inverse = sb("inverse", [P, TILES * 4])
        normed = sb("normed", [P, TILES, DIM])
        normedT = sb("normedT", [P, CC, CHUNK])
        y = sb("y", [P, TILES, DIM])
        maxima = sb("maxima", [P, TILES, HEADS])
        shift_rest = sb("shift_rest", [HEADS, CHUNK])
        shift_parts = sb("shift_parts", [HEADS, SHIFT_ROWS, CHUNK], bf16)
        scores = ctx.enter_context(nc.psum_tensor("scores", [P, 6 * CHUNK], f32))
        outs = ctx.enter_context(nc.psum_tensor("outs", [P, CHUNK], f32))
        misc = ctx.enter_context(nc.psum_tensor("misc", [P, CHUNK], f32))

        tables_ready, ones_ready, passed = sem("tables_ready"), sem("ones_ready"), sem("passed")
        keys_loaded = [sem(f"keys_loaded{q}") for q in range(QUADS)]
        q_loaded = [sem(f"q_loaded{u}") for u in range(2)]
        shift_loaded = [sem(f"shift_loaded{u}") for u in range(2)]
        index_q_loaded = [sem(f"index_q_loaded{p}") for p in range(2)]
        index_k_loaded, window_loaded, res_loaded = sem("index_k_loaded"), sem("window_loaded"), sem("res_loaded")
        scored, exps_done, probs_used = sem("scored"), sem("exps_done"), sem("probs_used")
        outs_saved = sem("outs_saved")
        misc_filled, misc_drained = sem("misc_filled"), sem("misc_drained")
        topk_step, topk_done = sem("topk_step"), sem("topk_done")
        inverse_ready, split_step, shift_split = sem("inverse_ready"), sem("split_step"), sem("shift_split")
        y_stored = sem("y_stored")
        all_scored, all_reduced, all_turned = sem("all_scored"), sem("all_reduced"), sem("all_turned")
        all_step, all_read, all_split, all_loaded = sem("all_step"), sem("all_read"), sem("all_split"), sem("all_loaded")
        block = ctx.enter_context(nc.Block())

        SCORE_BUFS, PROB_BUFS, SAVED = 3, 2, QUADS

        def jobs_before(n):
            return PRO_JOBS + n * NJOBS

        def quad_used(n, q):
            return PROB_BUFS + STEPS * n + KEY_TILES * (q + 1)

        def pro_job(kind, g, i=0):
            if kind == "index":
                return 4 * g + i if g < 2 else 8 + 17 + 6 * (g - 2) + 2 + i
            if kind == "window":
                return 8 + 4 * g + i
            if kind == "shift":
                return 8 + 16
            return 8 + 17 + 6 * g + i

        def stacked(dst, parts_dram, side, heads, cols):
            for slot, pair in enumerate(PAIRS):
                yield (dst[slot * HEAD_DIM:(slot + 1) * HEAD_DIM],
                       parts_dram[pair[side], heads.start * HEAD_DIM:heads.stop * HEAD_DIM, cols]
                       .rearrange("(h i) t -> i h t", i=HEAD_DIM))

        @block.sync
        def _(sp):
            def load_queries(chunk, u):
                for dst, src in stacked(queries[u], q_parts, 0, slice(0, HEADS), bass.ds(chunk * CHUNK, CHUNK)):
                    sp.dma_start(dst, src).then_inc(q_loaded[u], 16)

            def load_index_q(tile, p):
                sp.dma_start(index_q[p][:, :], index_qk[0:INDEX_DIM, bass.ds(tile * P, P)])\
                    .then_inc(index_q_loaded[p], 16)

            def load_shift(u, loaded):
                for j in range(SHIFT_ROWS):
                    sp.dma_start(queries[u][STACK + j:STACK + j + 1, :, :], shift_parts[:, j]).then_inc(loaded, 16)

            for g in range(2):
                load_index_q(g, g)
            load_queries(0, 0)
            sp.wait_ge(shift_split, 1)
            load_shift(0, shift_loaded[0])
            for g in range(2, INDEX_LEAD + 1):
                sp.wait_ge(misc_filled, pro_job("index", g - 2, 3) + 1)
                load_index_q(g, g % 2)
            use_all = sp.value_load(flag[0:1, 0:1], min_val=0, max_val=1)
            with sp.Fori(0, CHUNKS // 2) as m:
                for u in range(2):
                    n = 2 * m + u
                    with sp.If(use_all != 0):
                        sp.wait_ge(shift_loaded[u], 16 * SHIFT_ROWS * (m + 1))
                        sp.wait_ge(all_split, n + 1)
                        load_shift(u, all_loaded)
                    sp.wait_ge(y_stored, 16 * (n + 1))
                    sp.dma_start(y[:, :, :], residual[bass.ds(((n + CHUNKS - 1) % CHUNKS) * CHUNK, CHUNK)]
                                 .rearrange("(t p) d -> p t d", p=P)).then_inc(res_loaded, 16)
                    sp.wait_ge(probs_used, quad_used(n, -1))
                    load_queries((n + 1) % CHUNKS, 1 - u)
                    for t in range(TILES):
                        if t == 0:
                            sp.wait_ge(misc_filled, jobs_before(n))
                        else:
                            sp.wait_ge(misc_filled, jobs_before(n) + job_position("index", (t - 1, 3)) + 1)
                        load_index_q((TILES * n + t + INDEX_LEAD + 1) % (TOKENS // P), (t + 1) % 2)
                        if t == 0:
                            sp.wait_ge(misc_drained, jobs_before(n) + job_position("proj", 1) + 1)
                            stand(sp, passed)
                            with sp.If(n > 0):
                                sp.dma_start(out_rows[bass.ds(((n + CHUNKS - 1) % CHUNKS) * CHUNK, CHUNK)]
                                             .rearrange("(t p) d -> p t d", p=P), y[:, :, :]).then_inc(y_stored, 16)
                    sp.wait_ge(shift_split, n + 2)
                    load_shift(1 - u, shift_loaded[1 - u])
            sp.wait_ge(y_stored, 16 * (CHUNKS + 1))
            last_rows = slice((CHUNKS - 1) * CHUNK, CHUNKS * CHUNK)
            sp.dma_start(y[:, :, :], residual[last_rows].rearrange("(t p) d -> p t d", p=P)).then_inc(res_loaded, 16)
            sp.wait_ge(misc_drained, jobs_before(CHUNKS) + QUADS + CC + 2)
            sp.dma_start(out_rows[last_rows].rearrange("(t p) d -> p t d", p=P), y[:, :, :]).then_inc(y_stored, 16)
            sp.wait_ge(y_stored, 16 * (CHUNKS + 2))
            for u in range(2):
                sp.wait_ge(q_loaded[u], 16 * len(PAIRS) * (CHUNKS // 2 + (u == 0)))
                sp.wait_ge(shift_loaded[u], 16 * SHIFT_ROWS * (CHUNKS // 2 + (u == 0)))
            sp.wait_ge(index_q_loaded[0], 16 * (TOKENS // P // 2 + 4))
            sp.wait_ge(index_q_loaded[1], 16 * (TOKENS // P // 2 + 3))

        @block.gpsimd
        def _(pool):
            def load_index_k(b):
                pool.dma_start(index_k[:, :], index_qk[INDEX_DIM:P, bass.ds(b * SEQ, ASSOC)])\
                    .then_inc(index_k_loaded, 16)

            def load_window_keys(b):
                for dst, src in stacked(window_keys, k_parts, 1, slice(0, HEADS), bass.ds(b * SEQ + ASSOC, WINDOW)):
                    pool.dma_start(dst, src).then_inc(window_loaded, 16)

            def load_quad(b, q):
                heads = slice(4 * q, 4 * q + 4)
                for dst, src in stacked(keys[:, heads], k_parts, 1, heads, bass.ds(b * SEQ, SEQ)):
                    pool.dma_start(dst, src).then_inc(keys_loaded[q], 16)
                pool.dma_start(v_sb[:, q], values[bass.ds(b * SEQ, SEQ), q * 4 * V_COLS:(q + 1) * 4 * V_COLS]
                               .rearrange("(t p) c -> p t c", p=P)).then_inc(keys_loaded[q], 16)

            load_index_k(0)
            load_window_keys(0)
            for q in range(QUADS):
                load_quad(0, q)
            nc.gpsimd.memset(keys[STACK:ROWS].rearrange("p h t -> p (h t)").bitcast(f32), BF16_ONES)\
                .then_inc(ones_ready, 1)
            with pool.Fori(1, BATCH) as b:
                before = jobs_before(b * (CHUNKS // BATCH) - 2)
                pool.wait_ge(misc_filled, before + job_position("index", (1, 3)) + 1)
                load_index_k(b)
                pool.wait_ge(misc_filled, before + job_position("window", (TILES - 1, QUADS - 1)) + 1)
                load_window_keys(b)
                for q in range(QUADS):
                    pool.wait_ge(probs_used, quad_used(b * (CHUNKS // BATCH) - 1, q))
                    load_quad(b, q)
            before = jobs_before(CHUNKS - 2)
            pool.wait_ge(misc_filled, before + job_position("index", (1, 3)) + 1)
            load_index_k(0)
            pool.wait_ge(misc_filled, before + job_position("window", (TILES - 1, QUADS - 1)) + 1)
            load_window_keys(0)
            pool.wait_ge(index_k_loaded, 16 * (BATCH + 1))
            pool.wait_ge(window_loaded, 16 * len(PAIRS) * (BATCH + 1))

        @block.scalar
        def _(act):
            def drain_index(count, tile, p, i):
                act.wait_ge(misc_filled, count + 1)
                if i == 0 and not (isinstance(tile, int) and tile < 2):
                    act.wait_ge(topk_done, tile - 1)
                nc.scalar.activation(index_scores[p][:, i * PIECE:(i + 1) * PIECE], misc[:, 0:PIECE], ACT.Relu)\
                    .then_inc(misc_drained, 1)

            def drain_mask(count, u, t, i):
                act.wait_ge(misc_filled, count + 1)
                stand(act, passed)
                lo, hi = MASK_SPLIT[i], MASK_SPLIT[i + 1]
                nc.scalar.copy(masks[u][:, lo:hi, t * P:(t + 1) * P],
                               misc[:, :].bitcast(bf16)[:, 0:(hi - lo) * P].rearrange("p (a s) -> p a s", s=P),
                               saturate=False).then_inc(misc_drained, 1)

            def save_outs(n, q):
                act.wait_ge(probs_used, quad_used(n, q))
                act.wait_ge(misc_filled, jobs_before(n) + job_position("norm", q) + 1)
                nc.scalar.activation(heads_out[:, q], outs[:, :], ACT.Copy).then_inc(outs_saved, 1)

            act.wait_ge(tables_ready, 1)
            act.sem_inc(exps_done, SCORE_BUFS)
            act.sem_inc(outs_saved, SAVED)
            for g in range(2):
                for i in range(INDEX_PIECES):
                    drain_index(pro_job("index", g, i), g, g % 2, i)
            for g in range(MASK_LEAD):
                for i in range(2):
                    drain_mask(pro_job("mask", g, i), 0, g, i)
                for i in range(INDEX_PIECES):
                    drain_index(pro_job("index", g + 2, i), g + 2, g % 2, i)
            with act.Fori(0, CHUNKS // 2) as m:
                for u in range(2):
                    n = 2 * m + u
                    for s in range(STEPS):
                        for h in range(2):
                            act.wait_ge(scored, 2 * STEPS * n + 2 * s + h + 1)
                            if h == 0:
                                act.wait_ge(probs_used, STEPS * n + s + 1)
                            buf = (2 * s + h) % SCORE_BUFS
                            nc.scalar.activation(probs[s % 2][:, 2 * h:2 * h + 2],
                                                 scores[:, buf * 2 * CHUNK:(buf + 1) * 2 * CHUNK]
                                                 .rearrange("p (a s) -> p a s", a=2), ACT.Exp).then_inc(exps_done, 1)
                        if s % KEY_TILES == 0 and s > 0:
                            save_outs(n, s // KEY_TILES - 1)
                        if s in JOBS:
                            pos, kind, arg = JOBS[s]
                            if kind == "index":
                                t, i = arg
                                drain_index(jobs_before(n) + pos, TILES * n + t + INDEX_LEAD, t % 2, i)
                            elif kind == "mask":
                                drain_mask(jobs_before(n) + pos, 1 - u, *arg)
                    save_outs(n, QUADS - 1)

        @block.vector
        def _(dve):
            def topk_op(tile, p, r, before=None):
                if r < 2 * (TOPK // 8):
                    if r == 0:
                        dve.wait_ge(misc_drained, before)
                    else:
                        dve.wait_ge(topk_step, 2 * (TOPK // 8) * tile + r)
                    stand(dve, passed)
                    if r % 2 == 0:
                        nc.vector.max(top8[:, :], index_scores[p][:, :]).then_inc(topk_step, 1)
                    else:
                        nc.vector.match_replace(index_scores[p][:, :], top8[:, :], index_scores[p][:, :], -1.0)\
                            .then_inc(topk_step, 1)
                else:
                    dve.wait_ge(topk_step, 2 * (TOPK // 8) * (tile + 1))
                    nc.vector.tensor_scalar(left_out[:, :], index_scores[p][:, :], 0.0, None, ALU.is_ge)\
                        .then_inc(topk_done, 1)

            def drain_window(count, t, q):
                dve.wait_ge(misc_filled, count + 1)
                nc.vector.reduce_max(maxima[:, t, 4 * q:4 * q + 4], misc[:, :].rearrange("p (h w) -> p h w", h=4), AX.X)\
                    .then_inc(misc_drained, 1)

            def split_shift(step, before, read, read_before, done):
                nc.vector.tensor_scalar(shift_parts[:, 0], misc[0:HEADS, :], -1.0, None, ALU.mult).then_inc(step, 1)
                dve.wait_ge(step, before + 1)
                nc.vector.scalar_tensor_tensor(shift_rest[:, :], misc[0:HEADS, :], -1.0, shift_parts[:, 0],
                                               ALU.mult, ALU.subtract).then_inc(read, 1)
                dve.wait_ge(read, read_before + 1)
                nc.vector.tensor_copy(shift_parts[:, 1], shift_rest[:, :]).then_inc(step, 1)
                dve.wait_ge(step, before + 2)
                nc.vector.tensor_tensor(shift_parts[:, 2], shift_rest[:, :], shift_parts[:, 1], ALU.subtract)\
                    .then_inc(done, 1)

            def drain_norm(count, done, q):
                dve.wait_ge(misc_filled, count + 1)
                blocks = misc[:, :].rearrange("p (b c) -> p b c", c=32)
                nc.vector.reciprocal(inverse[:, :], blocks[:, :, HEAD_DIM]).then_inc(inverse_ready, 1)
                dve.wait_ge(inverse_ready, done + 1)
                nc.vector.tensor_tensor(
                    normed[:, :, 4 * q * HEAD_DIM:4 * (q + 1) * HEAD_DIM].rearrange("p t (h i) -> p t h i", h=4),
                    misc[:, :].rearrange("p (t h c) -> p t h c", t=TILES, h=4)[:, :, :, 0:HEAD_DIM],
                    inverse[:, :].rearrange("p (t h) -> p t h", h=4).unsqueeze(3)
                    .to_broadcast([P, TILES, 4, HEAD_DIM]), ALU.mult).then_inc(misc_drained, 1)

            def drain_turn(count, c):
                dve.wait_ge(misc_filled, count + 1)
                nc.vector.tensor_copy(normedT[:, c], misc[:, :]).then_inc(misc_drained, 1)

            def drain_proj(count, n, c):
                dve.wait_ge(misc_filled, count + 1)
                dve.wait_ge(res_loaded, 16 * (n + 1))
                part = y[:, 2 * c:2 * c + 2]
                nc.vector.tensor_tensor(part, misc[:, :].rearrange("p (t d) -> p t d", t=2), part, ALU.add)\
                    .then_inc(misc_drained, 1)

            nc.vector.memset(outs[:, :], 0.0).then_inc(tables_ready, 1)
            dve.wait_ge(tables_ready, 1)
            nc.vector.memset(heads_out[:, :, :], 1.0).then_inc(tables_ready, 1)
            dve.wait_ge(tables_ready, 2)
            dve.sem_inc(y_stored, 32)
            dve.sem_inc(probs_used, PROB_BUFS)
            dve.sem_inc(all_reduced, 1)
            for g in range(TOPK_LEAD):
                for r in range(2 * (TOPK // 8)):
                    topk_op(g, g % 2, r, pro_job("index", g, 3) + 1)
                if g > 0:
                    dve.wait_ge(misc_filled, pro_job("mask", g - 1, 1) + 1)
                topk_op(g, g % 2, 2 * (TOPK // 8))
                if g == 0:
                    for t in range(TILES):
                        for q in range(QUADS):
                            drain_window(pro_job("window", t, q), t, q)
                    dve.wait_ge(misc_filled, pro_job("shift", 0) + 1)
                    split_shift(split_step, 0, misc_drained, pro_job("shift", 0), shift_split)
            use_all = dve.value_load(flag[0:1, 0:1], min_val=0, max_val=1)
            with dve.Fori(0, CHUNKS // 2) as m:
                for u in range(2):
                    n = 2 * m + u
                    with dve.If(use_all != 0):
                        with dve.Fori(0, HEADS) as h:
                            for t in range(TILES):
                                dve.wait_ge(all_scored, TILES * HEADS * n + TILES * h + t + 1)
                                stand(dve, passed)
                                nc.vector.reduce_max(maxima[:, t, bass.ds(h, 1)], scores[:, 0:SEQ], AX.X)\
                                    .then_inc(all_reduced, 1)
                        dve.wait_ge(all_turned, n + 1)
                        dve.wait_ge(shift_loaded[u], 16 * SHIFT_ROWS * (m + 1))
                        split_shift(all_step, 2 * n, all_read, n, all_split)
                        dve.wait_ge(all_loaded, 16 * SHIFT_ROWS * (n + 1))
                        stand(dve, passed)
                    for s in range(STEPS):
                        t, r = divmod(s, WINDOW_STEPS)
                        if s in JOBS:
                            pos, kind, arg = JOBS[s]
                            count = jobs_before(n) + pos
                            if kind == "norm":
                                drain_norm(count, QUADS * n + arg, arg)
                            elif kind == "turn":
                                drain_turn(count, arg)
                            elif kind == "proj":
                                drain_proj(count, n, arg)
                            elif kind == "window":
                                drain_window(count, *arg)
                            elif kind == "shift":
                                dve.wait_ge(shift_loaded[u], 16 * SHIFT_ROWS * (m + 1))
                                dve.wait_ge(misc_filled, count + 1)
                                split_shift(split_step, 2 * (n + 1), misc_drained, count, shift_split)
                        tile, p = TILES * n + t + TOPK_LEAD, (t + TOPK_LEAD) % 2
                        topk_op(tile, p, r, jobs_before(n) + (0 if t == 0 else job_position("index", (t - 1, 3)) + 1))
                        if r == WINDOW_STEPS - 1:
                            dve.wait_ge(misc_filled, jobs_before(n) + job_position("mask", (t, 1)) + 1)
                            topk_op(tile, p, r + 1)
            last = jobs_before(CHUNKS)
            for q in range(QUADS):
                drain_norm(last + q, QUADS * CHUNKS + q, q)
            for c in range(CC):
                drain_turn(last + QUADS + c, c)
            for c in range(2):
                drain_proj(last + QUADS + CC + c, CHUNKS, c)

        @block.tensor
        def _(pe):
            def fill_index(count, tile, p, i, k_loads):
                pe.wait_ge(misc_drained, count) if not (isinstance(count, int) and count == 0) else None
                if i == 0:
                    pe.wait_ge(index_q_loaded[p], 16 * (tile // 2 + 1))
                    pe.wait_ge(index_k_loaded, 16 * k_loads)
                nc.tensor.matmul(misc[:, 0:PIECE], index_q[p][:, :], index_k[:, i * PIECE:(i + 1) * PIECE],
                                 start=True, stop=True).then_inc(misc_filled, 1)

            def fill_mask(count, tile, i):
                pe.wait_ge(misc_drained, count)
                pe.wait_ge(topk_done, tile + 1)
                lo, hi = MASK_SPLIT[i], MASK_SPLIT[i + 1]
                for a in range(lo, hi):
                    tr = nc.tensor.transpose(misc[:, :].bitcast(bf16)[:, (a - lo) * P:(a - lo + 1) * P],
                                             left_out[:, a * P:(a + 1) * P], ident_b[:, :])
                tr.then_inc(misc_filled, 1)

            def fill_window(count, u, t, q):
                pe.wait_ge(misc_drained, count)
                for j in range(4):
                    mm = nc.tensor.matmul(misc[:, j * WINDOW:(j + 1) * WINDOW],
                                          queries[u][0:STACK, 4 * q + j, t * P:(t + 1) * P],
                                          window_keys[0:STACK, 4 * q + j, :], start=True, stop=True)
                mm.then_inc(misc_filled, 1)

            def turn_maxima(signal):
                for t in range(TILES):
                    mm = nc.tensor.matmul(misc[0:HEADS, t * P:(t + 1) * P], maxima[:, t], ident[:, :],
                                          start=True, stop=True)
                mm.then_inc(signal, 1)

            def fill_norm(count, n, q):
                pe.wait_ge(misc_drained, count)
                pe.wait_ge(outs_saved, QUADS * n + q + 1)
                for t in range(TILES):
                    tr = nc.tensor.transpose(misc[:, t * P:(t + 1) * P], heads_out[:, q, t * P:(t + 1) * P], ident[:, :])
                tr.then_inc(misc_filled, 1)

            def fill_turn(count, c):
                pe.wait_ge(misc_drained, count)
                for t in range(TILES):
                    tr = nc.tensor.transpose(misc[:, t * P:(t + 1) * P], normed[:, t, c * P:(c + 1) * P], ident[:, :])
                tr.then_inc(misc_filled, 1)

            def fill_proj(count, half):
                pe.wait_ge(misc_drained, count)
                for j in range(2):
                    t = 2 * half + j
                    for c in range(CC):
                        mm = nc.tensor.matmul(misc[:, j * DIM:(j + 1) * DIM], normedT[:, c, t * P:(t + 1) * P],
                                              woT[:, c], start=c == 0, stop=c == CC - 1)
                mm.then_inc(misc_filled, 1)

            def weigh_values(n, s):
                q, kt = divmod(s, KEY_TILES)
                pe.wait_ge(exps_done, SCORE_BUFS + 2 * STEPS * n + 2 * s + 2)
                if kt == 0:
                    pe.wait_ge(outs_saved, SAVED + QUADS * n + q)
                for j in range(4):
                    mm = nc.tensor.matmul(outs[32 * j:32 * j + V_COLS, :], v_sb[:, q, kt, j * V_COLS:(j + 1) * V_COLS],
                                          probs[s % 2][:, j], start=kt == 0, stop=kt == KEY_TILES - 1)
                mm.then_inc(probs_used, 1)

            pe.wait_ge(tables_ready, 2)
            for g in range(2):
                for i in range(INDEX_PIECES):
                    fill_index(pro_job("index", g, i), g, g % 2, i, 1)
            pe.wait_ge(window_loaded, 16 * len(PAIRS))
            pe.wait_ge(q_loaded[0], 16 * len(PAIRS))
            for t in range(TILES):
                for q in range(QUADS):
                    fill_window(pro_job("window", t, q), 0, t, q)
            pe.wait_ge(misc_drained, pro_job("shift", 0))
            turn_maxima(misc_filled)
            for g in range(MASK_LEAD):
                for i in range(2):
                    fill_mask(pro_job("mask", g, i), g, i)
                for i in range(INDEX_PIECES):
                    fill_index(pro_job("index", g + 2, i), g + 2, g % 2, i, 1)
            pe.wait_ge(ones_ready, 1)
            use_all = pe.value_load(flag[0:1, 0:1], min_val=0, max_val=1)
            with pe.Fori(0, CHUNKS // 2) as m:
                for u in range(2):
                    n = 2 * m + u
                    pe.wait_ge(misc_drained, jobs_before(n))
                    pe.wait_ge(shift_loaded[u], 16 * SHIFT_ROWS * (m + 1))
                    with pe.If(use_all != 0):
                        for q in range(QUADS):
                            pe.wait_ge(keys_loaded[q], 16 * (len(PAIRS) + 1) * (n // (CHUNKS // BATCH) + 1))
                        pe.wait_ge(exps_done, SCORE_BUFS + 2 * STEPS * n)
                        stand(pe, passed)
                        with pe.Fori(0, HEADS) as h:
                            for t in range(TILES):
                                pe.wait_ge(all_reduced, TILES * HEADS * n + TILES * h + t + 1)
                                for c in range(SEQ // CHUNK):
                                    nc.tensor.matmul(scores[:, c * CHUNK:(c + 1) * CHUNK],
                                                     queries[u][0:STACK, bass.ds(h, 1), t * P:(t + 1) * P],
                                                     keys[0:STACK, bass.ds(h, 1), c * CHUNK:(c + 1) * CHUNK],
                                                     start=True, stop=False)
                                    blocks = range(4 * c, min(4 * c + 4, ASSOC_TILES))
                                    for a in blocks:
                                        mm = nc.tensor.matmul(scores[:, a * P:(a + 1) * P],
                                                              masks[u][:, a, t * P:(t + 1) * P], exclude_diag[:, :],
                                                              start=False, stop=a == blocks[-1])
                                mm.then_inc(all_scored, 1)
                        pe.wait_ge(all_reduced, TILES * HEADS * (n + 1) + 1)
                        turn_maxima(all_turned)
                        pe.wait_ge(all_loaded, 16 * SHIFT_ROWS * (n + 1))
                        stand(pe, passed)
                    for s in range(STEPS):
                        q, kt = divmod(s, KEY_TILES)
                        if kt == 0:
                            pe.wait_ge(keys_loaded[q], 16 * (len(PAIRS) + 1) * (n // (CHUNKS // BATCH) + 1))
                        for half in range(2):
                            i = 2 * s + half
                            buf = i % SCORE_BUFS
                            used = i - SCORE_BUFS if i >= SCORE_BUFS else (2 * STEPS - 1 - (2 * STEPS - 1 - i) % SCORE_BUFS) - 2 * STEPS
                            pe.wait_ge(exps_done, SCORE_BUFS + 2 * STEPS * n + used + 1)
                            for j in range(2):
                                head = 4 * q + 2 * half + j
                                bank = scores[:, (2 * buf + j) * CHUNK:(2 * buf + j + 1) * CHUNK]
                                mm = nc.tensor.matmul(bank, keys[0:ROWS, head, kt * P:(kt + 1) * P],
                                                      queries[u][0:ROWS, head, :], start=True, stop=kt >= ASSOC_TILES)
                                if kt < ASSOC_TILES:
                                    mm = nc.tensor.matmul(bank, exclude_diag[:, :], masks[u][:, kt, :],
                                                          start=False, stop=True)
                            mm.then_inc(scored, 1)
                        if s in JOBS:
                            pos, kind, arg = JOBS[s]
                            count = jobs_before(n) + pos
                            if kind == "index":
                                t, i = arg
                                loads = (n + 1 + (t >= 2)) // (CHUNKS // BATCH) + 1
                                fill_index(count, TILES * n + t + INDEX_LEAD, t % 2, i, loads)
                            elif kind == "mask":
                                fill_mask(count, TILES * n + arg[0] + MASK_LEAD, arg[1])
                            elif kind == "window":
                                if arg == (0, 0):
                                    pe.wait_ge(q_loaded[1 - u], 16 * len(PAIRS) * (m + u + 1))
                                    pe.wait_ge(window_loaded, 16 * len(PAIRS) * ((n + 1) // (CHUNKS // BATCH) + 1))
                                fill_window(count, 1 - u, *arg)
                            elif kind == "shift":
                                pe.wait_ge(misc_drained, count)
                                turn_maxima(misc_filled)
                            elif kind == "norm":
                                fill_norm(count, n, arg)
                            elif kind == "turn":
                                fill_turn(count, arg)
                            else:
                                fill_proj(count, arg)
                        if s > 0:
                            weigh_values(n, s - 1)
                    weigh_values(n, STEPS - 1)
            last = jobs_before(CHUNKS)
            for q in range(QUADS):
                fill_norm(last + q, CHUNKS, q)
            for c in range(CC):
                fill_turn(last + QUADS + c, c)
            for half in range(2):
                fill_proj(last + QUADS + CC + half, half)


_INS = ['L0_attn_x', 'L0_attn_wq', 'L0_attn_bq', 'L0_attn_wk', 'L0_attn_bk', 'L0_attn_wv', 'L0_attn_bv', 'L0_attn_wo',
        'L0_attn_bo', 'L0_attn_wqi', 'L0_attn_bqi', 'L0_attn_wki', 'L0_attn_bki', 'L0_ffn_Win', 'L0_ffn_bin_',
        'L0_ffn_W1', 'L0_ffn_b1', 'L0_ffn_W2', 'L0_ffn_b2', 'L0_ffn_Wout', 'L0_ffn_bout']
_OUTS = [((BATCH, SEQ, DIM), 'float32')]


def kernel(**inputs):
    import numpy as _np
    import concourse.bacc as _bacc
    from concourse import mybir as _mybir
    from concourse.bass_utils import run_bass_kernel_spmd as _run

    nc = _bacc.Bacc("TRN2", target_bir_lowering=False, num_devices=1)
    arrays, args = {}, []
    for name in _INS:
        a = _np.ascontiguousarray(inputs[name])
        arrays[f"in_{name}_dram"] = a
        args.append(nc.dram_tensor(f"in_{name}_dram", a.shape, _mybir.dt.from_np(a.dtype), kind="ExternalInput").ap())
    for i, (shape, dtype) in enumerate(_OUTS):
        dt = _mybir.dt.from_np(_np.dtype(dtype))
        args.append(nc.dram_tensor(f"out_{i}_dram", shape, dt, kind="ExternalOutput").ap())
    build(nc, *args)
    r = _run(nc, [arrays], core_ids=[0])
    got = tuple(r.results[0][f"out_{i}_dram"] for i in range(len(_OUTS)))
    return got[0]
```

```python
import concourse.bass as bass
from concourse import mybir
from contextlib import ExitStack

BATCH, SEQ, DIM = 4, 2048, 256
HEADS, HEAD_DIM = 16, 16
TOPK, WINDOW, INDEX_DIM = 64, 128, 64
FFN_M, FFN_INNER = 64, 16
EPS = 1e-5
P = 128

TOKENS = BATCH * SEQ
CHUNK = 512
CHUNKS = TOKENS // CHUNK
TILES = CHUNK // P
CC = DIM // P
ASSOC = SEQ - WINDOW
ASSOC_TILES = ASSOC // P
KEY_TILES = SEQ // P
QUADS = HEADS // 4
SCALE = 0.25
V_COLS = HEAD_DIM + 1

PAIRS = ((0, 0), (0, 1), (1, 0), (1, 1), (0, 2), (2, 0))
STACK = len(PAIRS) * HEAD_DIM
SHIFT_ROWS = 3
ROWS = STACK + SHIFT_ROWS
EXCLUDED = -1e30

SPREAD_LIMIT = 75.0
BF16_ONES = 1.0019378662109375

STEPS = QUADS * KEY_TILES
WINDOW_STEPS = STEPS // TILES


def misc_jobs():
    at = {}
    for i in range(TILES):
        at[i + (i > 1)] = ("norm", i)
    at[7], at[9] = ("turn", 0), ("turn", 1)
    at[12], at[14] = ("proj", 0), ("proj", 1)
    for t in range(TILES):
        for i, r in enumerate((2, 5, 8, 11)):
            at[WINDOW_STEPS * t + r] = ("index", (t, i))
        for i, r in enumerate((6, 13)):
            at[WINDOW_STEPS * t + r] = ("mask", (t, i))
    free = [s for s in range(WINDOW_STEPS - 1, 3 * WINDOW_STEPS) if s not in at]
    for i in range(TILES * QUADS):
        at[free[i]] = ("window", (i // QUADS, i % QUADS))
    at[3 * WINDOW_STEPS + 3] = ("shift", 0)
    return {s: (n, *at[s]) for n, s in enumerate(sorted(at))}


JOBS = misc_jobs()
NJOBS = len(JOBS)
INDEX_LEAD, TOPK_LEAD, MASK_LEAD = 6, 5, 4
INDEX_PIECES = 4
PIECE = ASSOC // INDEX_PIECES
MASK_SPLIT = (0, 8, ASSOC_TILES)
PRO_JOBS = INDEX_LEAD * INDEX_PIECES + MASK_LEAD * 2 + TILES * QUADS + 1


def stand(engine, passed):
    engine.sem_inc(passed, 1)


def job_position(kind, arg):
    return [n for n, k, a in JOBS.values() if (k, a) == (kind, arg)][0]


SELECT_JOBS = INDEX_LEAD * INDEX_PIECES + MASK_LEAD * 2


def pro_job(kind, g, i=0):
    if kind == "index":
        return 4 * g + i if g < 2 else 8 + 6 * (g - 2) + 2 + i
    if kind == "mask":
        return 8 + 6 * g + i
    return SELECT_JOBS + (4 * g + i if kind == "window" else TILES * QUADS)


def stacked(dst, parts_dram, side, heads, cols):
    for slot, pair in enumerate(PAIRS):
        yield (dst[slot * HEAD_DIM:(slot + 1) * HEAD_DIM],
               parts_dram[pair[side], heads.start * HEAD_DIM:heads.stop * HEAD_DIM, cols]
               .rearrange("(h i) t -> i h t", i=HEAD_DIM))


class Selection:

    def __init__(self, nc, ctx, index_qk, ident_b):
        f32, bf16, f8 = mybir.dt.float32, mybir.dt.bfloat16, mybir.dt.float8e4

        def sb(name, shape, dt=f32):
            return ctx.enter_context(nc.sbuf_tensor(name, shape, dt))

        def sem(name):
            return ctx.enter_context(nc.semaphore(name))

        self.nc, self.index_qk, self.ident_b = nc, index_qk, ident_b
        self.first_masks = sb("masks0", [P, ASSOC_TILES, CHUNK], f8)
        self.index_k = sb("index_k", [INDEX_DIM, ASSOC])
        self.index_q = [sb(f"index_q{p}", [INDEX_DIM, P]) for p in range(2)]
        self.index_scores = [sb(f"index_scores{p}", [P, ASSOC]) for p in range(2)]
        self.top8 = sb("top8", [P, 8])
        self.first_queries = sb("queries0", [P, HEADS, CHUNK], bf16)
        self.window_keys = sb("window_keys", [P, HEADS, WINDOW], bf16)
        self.q_loaded, self.window_loaded = sem("q_loaded0"), sem("window_loaded")
        self.left_out = sb("left_out", [P, ASSOC], bf16)
        self.misc = ctx.enter_context(nc.psum_tensor("misc", [P, CHUNK], f32))
        self.index_q_loaded = [sem(f"index_q_loaded{p}") for p in range(2)]
        self.index_k_loaded = sem("index_k_loaded")
        self.misc_filled, self.misc_drained = sem("misc_filled"), sem("misc_drained")
        self.topk_step, self.topk_done = sem("topk_step"), sem("topk_done")

    def load_index_q(self, sp, tile, p):
        sp.dma_start(self.index_q[p][:, :], self.index_qk[0:INDEX_DIM, bass.ds(tile * P, P)])\
            .then_inc(self.index_q_loaded[p], 16)

    def load_index_k(self, queue, b):
        queue.dma_start(self.index_k[:, :], self.index_qk[INDEX_DIM:P, bass.ds(b * SEQ, ASSOC)])\
            .then_inc(self.index_k_loaded, 16)

    def load_queries(self, sp, q_parts, dst, loaded, chunk):
        for rows, src in stacked(dst, q_parts, 0, slice(0, HEADS), bass.ds(chunk * CHUNK, CHUNK)):
            sp.dma_start(rows, src).then_inc(loaded, 16)

    def load_window_keys(self, pool, k_parts, b):
        for rows, src in stacked(self.window_keys, k_parts, 1, slice(0, HEADS), bass.ds(b * SEQ + ASSOC, WINDOW)):
            pool.dma_start(rows, src).then_inc(self.window_loaded, 16)

    def fill_index(self, pe, count, tile, p, i, k_loads):
        pe.wait_ge(self.misc_drained, count) if not (isinstance(count, int) and count == 0) else None
        if i == 0:
            pe.wait_ge(self.index_q_loaded[p], 16 * (tile // 2 + 1))
            pe.wait_ge(self.index_k_loaded, 16 * k_loads)
        self.nc.tensor.matmul(self.misc[:, 0:PIECE], self.index_q[p][:, :], self.index_k[:, i * PIECE:(i + 1) * PIECE],
                         start=True, stop=True).then_inc(self.misc_filled, 1)

    def fill_mask(self, pe, count, tile, i):
        pe.wait_ge(self.misc_drained, count)
        pe.wait_ge(self.topk_done, tile + 1)
        lo, hi = MASK_SPLIT[i], MASK_SPLIT[i + 1]
        for a in range(lo, hi):
            tr = self.nc.tensor.transpose(self.misc[:, :].bitcast(mybir.dt.bfloat16)[:, (a - lo) * P:(a - lo + 1) * P],
                                     self.left_out[:, a * P:(a + 1) * P], self.ident_b[:, :])
        tr.then_inc(self.misc_filled, 1)

    def drain_index(self, act, count, tile, p, i):
        act.wait_ge(self.misc_filled, count + 1)
        if i == 0 and not (isinstance(tile, int) and tile < 2):
            act.wait_ge(self.topk_done, tile - 1)
        self.nc.scalar.activation(self.index_scores[p][:, i * PIECE:(i + 1) * PIECE], self.misc[:, 0:PIECE], mybir.ActivationFunctionType.Relu)\
            .then_inc(self.misc_drained, 1)

    def drain_mask(self, act, passed, count, masks_u, t, i):
        act.wait_ge(self.misc_filled, count + 1)
        stand(act, passed)
        lo, hi = MASK_SPLIT[i], MASK_SPLIT[i + 1]
        self.nc.scalar.copy(masks_u[:, lo:hi, t * P:(t + 1) * P],
                       self.misc[:, :].bitcast(mybir.dt.bfloat16)[:, 0:(hi - lo) * P].rearrange("p (a s) -> p a s", s=P),
                       saturate=False).then_inc(self.misc_drained, 1)

    def topk_op(self, dve, passed, tile, p, r, before=None):
        if r < 2 * (TOPK // 8):
            if r == 0:
                dve.wait_ge(self.misc_drained, before)
            else:
                dve.wait_ge(self.topk_step, 2 * (TOPK // 8) * tile + r)
            stand(dve, passed)
            if r % 2 == 0:
                self.nc.vector.max(self.top8[:, :], self.index_scores[p][:, :]).then_inc(self.topk_step, 1)
            else:
                self.nc.vector.match_replace(self.index_scores[p][:, :], self.top8[:, :], self.index_scores[p][:, :], -1.0)\
                    .then_inc(self.topk_step, 1)
        else:
            dve.wait_ge(self.topk_step, 2 * (TOPK // 8) * (tile + 1))
            self.nc.vector.tensor_scalar(self.left_out[:, :], self.index_scores[p][:, :], 0.0, None, mybir.AluOpType.is_ge)\
                .then_inc(self.topk_done, 1)



def build(nc, x, wq, bq, wk, bk, wv, bv, wo, bo, wqi, bqi, wki, bki, Win, bin_, W1, b1, W2, b2, Wout, bout, out):
    f32, bf16, f8, i32 = mybir.dt.float32, mybir.dt.bfloat16, mybir.dt.float8e4, mybir.dt.int32
    ALU, ACT, AX = mybir.AluOpType, mybir.ActivationFunctionType, mybir.AxisListType

    x_rows = x.rearrange("b s d -> (b s) d")
    out_rows = out.rearrange("b s d -> (b s) d")
    q_parts = nc.dram_tensor("q_parts", (3, DIM, TOKENS), bf16, kind="Internal").ap()
    k_parts = nc.dram_tensor("k_parts", (3, DIM, TOKENS), bf16, kind="Internal").ap()
    values = nc.dram_tensor("values", (TOKENS, HEADS * V_COLS), f32, kind="Internal").ap()
    index_qk = nc.dram_tensor("index_qk", (2 * INDEX_DIM, TOKENS), f32, kind="Internal").ap()
    residual = nc.dram_tensor("residual", (TOKENS, DIM), f32, kind="Internal").ap()

    with ExitStack() as whole:
        ident = whole.enter_context(nc.sbuf_tensor("ident", [P, P], f32))
        ident_b = whole.enter_context(nc.sbuf_tensor("ident_b", [P, P], bf16))
        exclude_diag = whole.enter_context(nc.sbuf_tensor("exclude_diag", [P, P], bf16))
        woT = whole.enter_context(nc.sbuf_tensor("woT", [P, CC, DIM], f32))
        flag = whole.enter_context(nc.sbuf_tensor("flag", [1, 1], i32))
        select = Selection(nc, whole, index_qk, ident_b)
        phase_one(nc, select, x_rows, wq, bq, wk, bk, wv, bv, wo, bo, wqi, bqi, wki, bki, Win, bin_, W1, b1, W2, b2,
                  Wout, bout, q_parts, k_parts, values, index_qk, residual,
                  ident, ident_b, exclude_diag, woT, flag)
        phase_two(nc, select, q_parts, k_parts, values, index_qk, residual, out_rows,
                  ident, ident_b, exclude_diag, woT, flag)


def phase_one(nc, select, x_rows, wq, bq, wk, bk, wv, bv, wo, bo, wqi, bqi, wki, bki, Win, bin_, W1, b1, W2, b2,
              Wout, bout, q_parts, k_parts, values, index_qk, residual,
              ident, ident_b, exclude_diag, woT, flag):
    f32, bf16, i32 = mybir.dt.float32, mybir.dt.bfloat16, mybir.dt.int32
    ALU, ACT, AX = mybir.AluOpType, mybir.ActivationFunctionType, mybir.AxisListType
    PAIRS_J = FFN_INNER // 2

    OUTS = [("xT0", "act"), ("xT1", "act"), ("s", "act"), ("q0", "dve"), ("q1", "dve"), ("k0", "dve"),
            ("k1", "dve"), ("v0", "dve"), ("v1", "dve"), ("index", "act"), ("norms", "dve"), ("g", "act"),
            ("ffn0", "dve"), ("ffn1", "dve")]
    NAMES = [n for n, _ in OUTS]
    RING = 7
    BESIDE = CHUNKS // BATCH
    OPS = 2 * (TOPK // 8) + 1
    ACT_FREES = ["xT0", "xT1", "s", "index", "g"]
    DVE_FREES = ["q0", "q1", "k0", "k1", "v0", "v1", "norms", "ffn0", "ffn1"]

    with ExitStack() as ctx:
        def sb(name, shape, dt=f32):
            return ctx.enter_context(nc.sbuf_tensor(name, shape, dt))

        def sem(name):
            return ctx.enter_context(nc.semaphore(name))

        w_nat = sb("w_nat", [P, 4, CC, DIM])
        wi_nat = sb("wi_nat", [P, DIM])
        wT = sb("wT", [P, 3, CC, DIM])
        wiT = sb("wiT", [P, CC, P])
        win = sb("win", [P, CC, 2, FFN_M])
        wout = sb("wout", [P, DIM])
        bq_raw = sb("bq_raw", [P, CC])
        bq_c = sb("bq_c", [P, CC])
        bk_c = sb("bk_c", [P, CC])
        bi_c = sb("bi_c", [P, 1])
        bin_c = sb("bin_c", [P, 1])
        b2_c = sb("b2_c", [P, 1])
        w1_c = sb("w1_c", [P, PAIRS_J])
        b1_c = sb("b1_c", [P, PAIRS_J])
        w2_c = sb("w2_c", [P, PAIRS_J])
        rows = sb("rows", [1, 3, DIM])
        ones = sb("ones", [1, P])
        bv_b = sb("bv_b", [P, DIM])
        bo_b = sb("bo_b", [P, DIM])
        ident2 = sb("ident2", [P, FFN_M])
        w2_diag = sb("w2_diag", [P, PAIRS_J, FFN_M])
        head_sum = sb("head_sum", [P, 8])
        head_sel = sb("head_sel", [P, 32], bf16)

        x_in = sb("x_in", [P, 2, TILES, DIM])
        stats = sb("stats", [P, TILES, 6])
        mean_var = sb("mean_var", [P, TILES, 2])
        var_eps = sb("var_eps", [P, TILES])
        std = sb("std", [P, TILES])
        rstd = sb("rstd", [P, TILES])
        xn = sb("xn", [P, TILES, DIM])
        xnT = sb("xnT", [P, CC, CHUNK])
        parts = sb("parts", [P, 2, CC, 3, CHUNK], bf16)
        rest = sb("rest", [P, 2, CC, CHUNK])
        squares = sb("squares", [P, 2, CC, CHUNK], bf16)
        v_out = sb("v_out", [P, TILES, HEADS, V_COLS])
        i_out = sb("i_out", [P, CHUNK])
        sT = sb("sT", [P, CHUNK])
        hidden = sb("hidden", [P, PAIRS_J, CHUNK])
        gT = sb("gT", [P, CHUNK])
        res = sb("res", [P, TILES, DIM])
        norm_now = sb("norm_now", [P, 1])
        norm_max = sb("norm_max", [P, 1])
        norm_row = sb("norm_row", [1, P])
        bound = sb("bound", [1, P // 2])
        bound_max = sb("bound_max", [1, 1])
        over = sb("over", [1, 1])
        bank = [ctx.enter_context(nc.psum_tensor(f"bank{i}", [P, CHUNK], f32)) for i in range(RING)]

        w_loaded, ffn_loaded = sem("w_loaded"), sem("ffn_loaded")
        x_loaded = [sem(f"x_loaded{u}") for u in range(2)]
        ident_ready, setup_dve, setup_pe = sem("ident_ready"), sem("setup_dve"), sem("setup_pe")
        norm_step, std_ready, xn_ready = sem("norm_step"), sem("std_ready"), sem("xn_ready")
        pe_out, act_freed, dve_freed = sem("pe_out"), sem("act_freed"), sem("dve_freed")
        first_part, hidden_ready, max_kept = sem("first_part"), sem("hidden_ready"), sem("max_kept")
        second_part, third_part, res_ready = sem("second_part"), sem("third_part"), sem("res_ready")
        parts_stored, v_stored, i_stored, res_stored = (sem("parts_stored"), sem("v_stored"), sem("i_stored"),
                                                        sem("res_stored"))
        final, passed = sem("final"), sem("passed")
        TABLES, FFN_TABLES = 20, 6
        block = ctx.enter_context(nc.Block())

        BESIDE_JOBS = {4 * g + i: ("index", g, i) for g in range(2) for i in range(INDEX_PIECES)}
        for g in range(MASK_LEAD):
            for i in range(2):
                BESIDE_JOBS[4 + OPS * (g + 1) + 4 + i] = ("mask", g, i)
            for i in range(INDEX_PIECES):
                BESIDE_JOBS[4 + OPS * (g + 1) + 6 + i] = ("index", g + 2, i)

        def slot(k, point):
            return 8 * (k - BESIDE) + point if isinstance(k, int) else None

        def out_bank(name):
            return bank[NAMES.index(name) % RING]

        def filled(name, k):
            return k * len(OUTS) + NAMES.index(name) + 1

        def act_count(name, k):
            return len(ACT_FREES) * (k + 1) + ACT_FREES.index(name) + 1

        def dve_count(name, k):
            return len(DVE_FREES) * (k + 1) + DVE_FREES.index(name) + 1

        @block.sync
        def _(sp):
            for i, w in enumerate((wq, wk, wv, wo)):
                sp.dma_start(w_nat[:, i], w.rearrange("(t p) c -> p t c", p=P)).then_inc(w_loaded, 16)
            sp.dma_start(wi_nat[0:INDEX_DIM], wqi).then_inc(w_loaded, 16)
            sp.dma_start(wi_nat[INDEX_DIM:P], wki).then_inc(w_loaded, 16)
            sp.dma_start(x_in[:, 0], x_rows[0:CHUNK].rearrange("(t p) d -> p t d", p=P)).then_inc(x_loaded[0], 16)
            for i, b in enumerate((bv, bo, bout)):
                sp.dma_start(rows[:, i], b.rearrange("(o n) -> o n", o=1)).then_inc(w_loaded, 16)
            sp.dma_start(bi_c[0:INDEX_DIM], bqi.rearrange("(p o) -> p o", o=1)).then_inc(w_loaded, 16)
            sp.dma_start(bi_c[INDEX_DIM:P], bki.rearrange("(p o) -> p o", o=1)).then_inc(w_loaded, 16)
            sp.wait_ge(setup_dve, 1)
            sp.dma_start(b2_c[0:FFN_M], b2.rearrange("(p o) -> p o", o=1)).then_inc(w_loaded, 16)
            sp.dma_start(x_in[:, 1], x_rows[CHUNK:2 * CHUNK].rearrange("(t p) d -> p t d", p=P)).then_inc(x_loaded[1], 16)
            def block_of(k, m, u):
                rows_k = bass.ds(k * CHUNK, CHUNK)
                if isinstance(k, int):
                    if k == BESIDE:
                        sp.wait_ge(i_stored, 16 * (BESIDE + 1))
                        sp.wait_ge(parts_stored, 64 * (BESIDE + 1))
                        select.load_queries(sp, q_parts, select.first_queries, select.q_loaded, 0)
                        for g in range(2):
                            select.load_index_q(sp, g, g)
                    for g in range(2, INDEX_LEAD + 1):
                        if k == {2: 5, 3: 5, 4: 8, 5: 10, 6: 13}[g]:
                            sp.wait_ge(select.misc_filled, pro_job("index", g - 2, 3) + 1)
                            select.load_index_q(sp, g, g % 2)
                sp.wait_ge(res_ready, k + 1)
                sp.wait_ge(xn_ready, k + 1)
                after = (k + 2) % CHUNKS
                sp.dma_start(x_in[:, u], x_rows[bass.ds(after * CHUNK, CHUNK)].rearrange("(t p) d -> p t d", p=P))\
                    .then_inc(x_loaded[u], 16)
                for i, dst in enumerate((q_parts, k_parts)):
                    for c in range(CC):
                        sp.wait_ge(third_part, 4 * k + 2 * i + c + 1)
                        sp.dma_start(dst[:, c * P:(c + 1) * P, rows_k].rearrange("j d t -> d j t"),
                                     parts[:, i, c]).then_inc(parts_stored, 16)
                sp.wait_ge(dve_freed, dve_count("v1", k))
                sp.dma_start(values[rows_k].rearrange("(t p) c -> p t c", p=P),
                             v_out[:, :, :, :].rearrange("p t h v -> p t (h v)")).then_inc(v_stored, 16)
                sp.wait_ge(act_freed, act_count("index", k))
                stand(sp, passed)
                sp.dma_start(index_qk[:, rows_k], i_out[:, :]).then_inc(i_stored, 16)
                sp.wait_ge(dve_freed, dve_count("ffn1", k))
                sp.dma_start(residual[rows_k].rearrange("(t p) d -> p t d", p=P), res[:, :, :])\
                    .then_inc(res_stored, 16)

            with sp.Fori(0, BESIDE // 2) as m:
                for u in range(2):
                    block_of(2 * m + u, m, u)
            for k in range(BESIDE, CHUNKS):
                block_of(k, k // 2, k % 2)
            sp.wait_ge(parts_stored, 64 * (CHUNKS + 1))
            sp.wait_ge(v_stored, 16 * (CHUNKS + 1))
            sp.wait_ge(i_stored, 16 * (CHUNKS + 1))
            sp.wait_ge(res_stored, 16 * (CHUNKS + 1))
            for u in range(2):
                sp.wait_ge(x_loaded[u], 16 * (CHUNKS // 2 + 1))

        @block.gpsimd
        def _(pool):
            nc.gpsimd.memset(ident[:], 0.0).then_inc(ident_ready, 1)
            pool.wait_ge(ident_ready, 1)
            nc.gpsimd.affine_select(out=ident[:], in_=ident[:], compare_op=ALU.not_equal, fill=1.0, base=0,
                                    pattern=[[-1, P]], channel_multiplier=1).then_inc(ident_ready, 1)
            nc.gpsimd.memset(v_out[:], 1.0).then_inc(ident_ready, 1)
            pool.wait_ge(setup_dve, 2)
            def block_of(k, m, u):
                if isinstance(k, int) and k == BESIDE:
                    pool.wait_ge(i_stored, 16 * (BESIDE + 1))
                    select.load_index_k(pool, 0)
                    pool.wait_ge(parts_stored, 64 * (BESIDE + 1))
                    select.load_window_keys(pool, k_parts, 0)
                pool.wait_ge(x_loaded[u], 16 * (m + 1))
                pool.wait_ge(res_stored, 16 * (k + 1))
                nc.gpsimd.tensor_tensor(res[:, :, :], x_in[:, u],
                                        bo_b[:, :].unsqueeze(1).to_broadcast([P, TILES, DIM]), ALU.add)\
                    .then_inc(res_ready, 1)
                for i in range(2):
                    for c in range(CC):
                        n = 4 * k + 2 * i + c
                        pool.wait_ge(dve_freed, dve_count(f"{'qk'[i]}{c}", k))
                        stand(pool, passed)
                        nc.gpsimd.tensor_copy(parts[:, i, c, 1], rest[:, i, c]).then_inc(second_part, 1)
                        pool.wait_ge(second_part, n + 1)
                        nc.gpsimd.tensor_tensor(parts[:, i, c, 2], rest[:, i, c], parts[:, i, c, 1],
                                                ALU.subtract).then_inc(third_part, 1)

            with pool.Fori(0, BESIDE // 2) as m:
                for u in range(2):
                    block_of(2 * m + u, m, u)
            for k in range(BESIDE, CHUNKS):
                block_of(k, k // 2, k % 2)

        @block.scalar
        def _(act):
            for i in range(2):
                act.dma_start(win[:, :, i], Win.rearrange("(t p) m -> p t m", p=P)).then_inc(w_loaded, 16)
                half = slice(i * FFN_M, (i + 1) * FFN_M)
                act.dma_start(wout[half], Wout).then_inc(w_loaded, 16)
                act.dma_start(bin_c[half], bin_.rearrange("(p o) -> p o", o=1)).then_inc(w_loaded, 16)
            act.dma_start(bq_raw[:, :], bq.rearrange("(t p) -> p t", p=P), allow_slow_non_contiguous=True).then_inc(w_loaded, 16)
            act.dma_start(bk_c[:, :], bk.rearrange("(t p) -> p t", p=P), allow_slow_non_contiguous=True).then_inc(w_loaded, 16)
            for i in range(2):
                half = slice(i * FFN_M, (i + 1) * FFN_M)
                js = slice(i * PAIRS_J, (i + 1) * PAIRS_J)
                act.dma_start(w1_c[half], W1[:, js]).then_inc(ffn_loaded, 16)
                act.dma_start(b1_c[half], b1[:, js]).then_inc(ffn_loaded, 16)
                act.dma_start(w2_c[half], W2[:, js]).then_inc(ffn_loaded, 16)
            act.sem_inc(act_freed, len(ACT_FREES))
            act.sem_inc(parts_stored, 64)
            act.sem_inc(i_stored, 16)
            act.wait_ge(setup_dve, 2)
            act.wait_ge(w_loaded, 16 * TABLES)
            act.wait_ge(ffn_loaded, 16 * FFN_TABLES)
            act.wait_ge(norm_step, 3)
            nc.scalar.activation(std[:, :], var_eps[:, :], ACT.Sqrt).then_inc(std_ready, 1)
            def beside(k, point):
                if slot(k, point) in BESIDE_JOBS:
                    kind, g, i = BESIDE_JOBS[slot(k, point)]
                    if kind == "index":
                        select.drain_index(act, pro_job(kind, g, i), g, g % 2, i)
                    else:
                        select.drain_mask(act, passed, pro_job(kind, g, i), select.first_masks, g, i)

            def block_of(k, m, u):
                for c in range(CC):
                    act.wait_ge(pe_out, filled(f"xT{c}", k))
                    nc.scalar.activation(xnT[:, c], out_bank(f"xT{c}")[:, :], ACT.Identity).then_inc(act_freed, 1)
                act.wait_ge(pe_out, filled("s", k))
                nc.scalar.activation(sT[:, :], out_bank("s")[:, :], ACT.Identity, bias=bin_c[:, 0:1])\
                    .then_inc(act_freed, 1)
                act.wait_ge(act_freed, act_count("s", k))
                beside(k, 0)
                for i, (name, b) in enumerate((("q", bq_c), ("k", bk_c))):
                    for c in range(CC):
                        act.wait_ge(pe_out, filled(f"{name}{c}", k))
                        if i == 0 and c == 0:
                            act.wait_ge(parts_stored, 64 * (k + 1))
                        src = out_bank(f"{name}{c}")
                        nc.scalar.activation(parts[:, i, c, 0], src[:, :], ACT.Identity, bias=b[:, c:c + 1])
                        if i == 0:
                            sq = nc.scalar.activation(squares[:, i, c], src[:, :], ACT.Square, bias=b[:, c:c + 1])
                        else:
                            sq = nc.scalar.activation(squares[:, i, c], src[:, :], ACT.Square)
                        sq.then_inc(first_part, 1)
                        for j in range(2 * (2 * i + c), 2 * (2 * i + c) + 2):
                            h = nc.scalar.activation(hidden[:, j], sT[:, :], ACT.Relu, bias=b1_c[:, j:j + 1],
                                                     scale=w1_c[:, j:j + 1])
                        beside(k, 1 + 2 * i + c)
                h.then_inc(hidden_ready, 1)
                act.wait_ge(norm_step, 4 * (k + 1) + 3)
                nc.scalar.activation(std[:, :], var_eps[:, :], ACT.Sqrt).then_inc(std_ready, 1)
                for point in (5, 6):
                    beside(k, point)
                act.wait_ge(pe_out, filled("index", k))
                act.wait_ge(i_stored, 16 * (k + 1))
                nc.scalar.activation(i_out[:, :], out_bank("index")[:, :], ACT.Identity, bias=bi_c[:, 0:1])\
                    .then_inc(act_freed, 1)
                beside(k, 7)
                act.wait_ge(pe_out, filled("g", k))
                nc.scalar.activation(gT[:, :], out_bank("g")[:, :], ACT.Identity, bias=b2_c[:, 0:1])\
                    .then_inc(act_freed, 1)

            with act.Fori(0, BESIDE // 2) as m:
                for u in range(2):
                    block_of(2 * m + u, m, u)
            for k in range(BESIDE, CHUNKS):
                block_of(k, k // 2, k % 2)

        @block.vector
        def _(dve):
            chain = [0]

            def step(ins):
                chain[0] += 1
                ins.then_inc(final, 1)
                dve.wait_ge(final, chain[0])

            nc.vector.memset(b2_c[:], 0.0).then_inc(setup_dve, 1)
            nc.vector.memset(ones[:], 1.0)
            nc.vector.memset(norm_max[:], 0.0)
            step(nc.vector.memset(head_sel[:], 0.0))
            dve.wait_ge(ident_ready, 3)
            nc.vector.tensor_copy(ident_b[:], ident[:])
            nc.vector.tensor_scalar(exclude_diag[:], ident[:], EXCLUDED, None, ALU.mult)
            nc.vector.tensor_tensor(ident2[:], ident[:, 0:FFN_M], ident[:, FFN_M:P], ALU.add)
            step(nc.vector.reduce_sum(head_sum[:], ident[:, :].rearrange("p (h i) -> p h i", i=HEAD_DIM), AX.X))
            step(nc.vector.tensor_copy(head_sel[:, 0:8], head_sum[:]))
            dve.wait_ge(w_loaded, 16 * TABLES)
            dve.wait_ge(ffn_loaded, 16 * FFN_TABLES)
            for j in range(PAIRS_J):
                nc.vector.tensor_scalar(w2_diag[:, j], ident2[:], w2_c[:, j:j + 1], None, ALU.mult)
            nc.vector.tensor_scalar(bq_c[:], bq_raw[:], SCALE, None, ALU.mult)
            dve.wait_ge(setup_pe, 1)
            for i in range(4):
                dst = woT if i == 3 else wT[:, i]
                nc.vector.tensor_scalar(dst[:, :, :], bank[i][:, :].rearrange("p (c n) -> p c n", c=CC),
                                        SCALE if i == 0 else 1.0, None, ALU.mult)
            nc.vector.tensor_copy(wiT[:, :, :], bank[4][:, 0:DIM].rearrange("p (c n) -> p c n", c=CC))
            nc.vector.tensor_copy(bv_b[:], bank[5][:, 0:DIM])
            step(nc.vector.tensor_copy(bo_b[:], bank[6][:, 0:DIM]))
            dve.sem_inc(dve_freed, len(DVE_FREES))
            dve.sem_inc(v_stored, 16)
            dve.sem_inc(res_stored, 16)
            dve.sem_inc(setup_dve, 1)

            def take_moments(k, u, loads):
                dve.wait_ge(x_loaded[u], 16 * loads)
                for t in range(TILES):
                    s = nc.vector.bn_stats(stats[:, t], x_in[:, u, t])
                s.then_inc(norm_step, 1)
                dve.wait_ge(norm_step, 4 * k + 1)
                stand(dve, passed)
                for t in range(TILES):
                    s = nc.vector.bn_aggr(mean_var[:, t], stats[:, t])
                s.then_inc(norm_step, 1)
                dve.wait_ge(norm_step, 4 * k + 2)
                nc.vector.tensor_scalar(var_eps[:, :], mean_var[:, :, 1], EPS, None, ALU.add).then_inc(norm_step, 1)

            def normalise(k, u):
                dve.wait_ge(std_ready, k + 1)
                nc.vector.reciprocal(rstd[:, :], std[:, :]).then_inc(norm_step, 1)
                dve.wait_ge(norm_step, 4 * k + 4)
                for t in range(TILES):
                    s = nc.vector.tensor_scalar(xn[:, t], x_in[:, u, t], mean_var[:, t, 0:1], rstd[:, t:t + 1],
                                                ALU.subtract, ALU.mult)
                s.then_inc(xn_ready, 1)

            take_moments(0, 0, 1)
            normalise(0, 0)

            def beside(k, point):
                if isinstance(k, int) and 0 <= slot(k, point) - 4 < TOPK_LEAD * OPS:
                    g, r = divmod(slot(k, point) - 4, OPS)
                    if r == OPS - 1 and g > 0:
                        dve.wait_ge(select.misc_filled, pro_job("mask", g - 1, 1) + 1)
                    select.topk_op(dve, passed, g, g % 2, r, pro_job("index", g, 3) + 1)

            def block_of(k, m, u):
                beside(k, 0)
                for i, (name, b) in enumerate((("q", bq_c), ("k", bk_c))):
                    for c in range(CC):
                        n = 4 * k + 2 * i + c
                        dve.wait_ge(first_part, n + 1)
                        if i == 0 and c == 0:
                            dve.wait_ge(parts_stored, 64 * (k + 1))
                        nc.vector.scalar_tensor_tensor(rest[:, i, c], out_bank(f"{name}{c}")[:, :], b[:, c:c + 1],
                                                       parts[:, i, c, 0], ALU.add, ALU.subtract)\
                            .then_inc(dve_freed, 1)
                        beside(k, 1 + 2 * i + c)
                    if i == 0:
                        take_moments(k + 1, 1 - u, m + u + 1)
                for c in range(2):
                    dve.wait_ge(pe_out, filled(f"v{c}", k))
                    if c == 0:
                        dve.wait_ge(v_stored, 16 * (k + 1))
                    nc.vector.tensor_tensor(
                        v_out[:, 2 * c:2 * c + 2, :, 0:HEAD_DIM],
                        out_bank(f"v{c}")[:, :].rearrange("p (t h i) -> p t h i", t=2, h=HEADS),
                        bv_b[:, :].rearrange("p (h i) -> p h i", h=HEADS).unsqueeze(1)
                        .to_broadcast([P, 2, HEADS, HEAD_DIM]), ALU.add).then_inc(dve_freed, 1)
                    if c == 0:
                        normalise(k + 1, 1 - u)
                    beside(k, 5 + c)
                dve.wait_ge(pe_out, filled("norms", k))
                nc.vector.reduce_max(norm_now[:, :], out_bank("norms")[:, :], AX.X)\
                    .then_inc(dve_freed, 1)
                dve.wait_ge(dve_freed, dve_count("norms", k))
                nc.vector.tensor_tensor(norm_max[:, :], norm_max[:, :], norm_now[:, :], ALU.max).then_inc(max_kept, 1)
                for c in range(2):
                    dve.wait_ge(pe_out, filled(f"ffn{c}", k))
                    if c == 0:
                        dve.wait_ge(res_ready, k + 1)
                    part = res[:, 2 * c:2 * c + 2]
                    nc.vector.tensor_tensor(part, out_bank(f"ffn{c}")[:, :].rearrange("p (t d) -> p t d", t=2),
                                            part, ALU.add).then_inc(dve_freed, 1)
                beside(k, 7)

            with dve.Fori(0, BESIDE // 2) as m:
                for u in range(2):
                    block_of(2 * m + u, m, u)
            for k in range(BESIDE, CHUNKS):
                block_of(k, k // 2, k % 2)
            dve.wait_ge(setup_pe, 2)
            step(nc.vector.tensor_copy(norm_row[:], bank[0][0:1, 0:P]))
            step(nc.vector.tensor_tensor(bound[:], norm_row[:, 0:P // 2], norm_row[:, P // 2:P], ALU.mult))
            step(nc.vector.reduce_max(bound_max[:], bound[:], AX.X))
            step(nc.vector.tensor_scalar(over[:], bound_max[:], (SPREAD_LIMIT / 2) ** 2, None, ALU.is_gt))
            step(nc.vector.tensor_copy(flag[:], over[:]))

        @block.tensor
        def _(pe):
            pe.wait_ge(ident_ready, 2)
            pe.wait_ge(w_loaded, 16 * TABLES)
            pe.wait_ge(final, 1)
            for i in range(4):
                for c in range(CC):
                    for o in range(CC):
                        nc.tensor.transpose(bank[i][:, c * DIM + o * P:c * DIM + (o + 1) * P],
                                            w_nat[:, i, o, c * P:(c + 1) * P], ident[:])
            for c in range(CC):
                nc.tensor.transpose(bank[4][:, c * P:(c + 1) * P], wi_nat[:, c * P:(c + 1) * P], ident[:])
            nc.tensor.matmul(bank[5][:, 0:DIM], ones[:, :], rows[:, 0], start=True, stop=True)
            nc.tensor.matmul(bank[6][:, 0:DIM], ones[:, :], rows[:, 1], start=True, stop=False)
            nc.tensor.matmul(bank[6][:, 0:DIM], ones[:, :], rows[:, 2], start=False, stop=True).then_inc(setup_pe, 1)
            pe.wait_ge(setup_dve, 2)

            def bank_free(name, k):
                i = NAMES.index(name)
                before, kb = (NAMES[i - RING], k) if i >= RING else (NAMES[i + RING], k - 1)
                if dict(OUTS)[before] == "act":
                    pe.wait_ge(act_freed, act_count(before, kb))
                else:
                    pe.wait_ge(dve_freed, dve_count(before, kb))

            def beside(k, point):
                if slot(k, point) in BESIDE_JOBS:
                    kind, g, i = BESIDE_JOBS[slot(k, point)]
                    if kind == "index":
                        select.fill_index(pe, pro_job(kind, g, i), g, g % 2, i, 1)
                    else:
                        select.fill_mask(pe, pro_job(kind, g, i), g, i)

            def block_of(k, m, u):
                pe.wait_ge(xn_ready, k + 1)
                for c in range(CC):
                    bank_free(f"xT{c}", k)
                    for t in range(TILES):
                        tr = nc.tensor.transpose(out_bank(f"xT{c}")[:, t * P:(t + 1) * P],
                                                 xn[:, t, c * P:(c + 1) * P], ident[:])
                    tr.then_inc(pe_out, 1)
                pe.wait_ge(act_freed, act_count("xT1", k))
                bank_free("s", k)
                for c in range(CC):
                    mm = nc.tensor.matmul(out_bank("s")[:, :], win[:, c].rearrange("p a m -> p (a m)"), xnT[:, c],
                                          start=c == 0, stop=c == CC - 1)
                mm.then_inc(pe_out, 1)
                beside(k, 0)
                for i, name in enumerate("qk"):
                    for o in range(CC):
                        bank_free(f"{name}{o}", k)
                        for c in range(CC):
                            mm = nc.tensor.matmul(out_bank(f"{name}{o}")[:, :], wT[:, i, c, o * P:(o + 1) * P],
                                                  xnT[:, c], start=c == 0, stop=c == CC - 1)
                        mm.then_inc(pe_out, 1)
                        beside(k, 1 + 2 * i + o)
                for o in range(2):
                    bank_free(f"v{o}", k)
                    for j in range(2):
                        t = 2 * o + j
                        for c in range(CC):
                            mm = nc.tensor.matmul(out_bank(f"v{o}")[:, j * DIM:(j + 1) * DIM],
                                                  xnT[:, c, t * P:(t + 1) * P], wT[:, 2, c],
                                                  start=c == 0, stop=c == CC - 1)
                    mm.then_inc(pe_out, 1)
                    beside(k, 5 + o)
                bank_free("index", k)
                for c in range(CC):
                    mm = nc.tensor.matmul(out_bank("index")[:, :], wiT[:, c], xnT[:, c],
                                          start=c == 0, stop=c == CC - 1)
                mm.then_inc(pe_out, 1)
                bank_free("norms", k)
                pe.wait_ge(first_part, 4 * k + 4)
                for i in range(2):
                    for c in range(CC):
                        q = 32 * (2 * i + c)
                        mm = nc.tensor.matmul(out_bank("norms")[q:q + 32, :], head_sel[:, :], squares[:, i, c],
                                              start=True, stop=True)
                mm.then_inc(pe_out, 1)
                beside(k, 7)
                bank_free("g", k)
                pe.wait_ge(hidden_ready, k + 1)
                for j in range(PAIRS_J):
                    q = FFN_M * (j % 2)
                    mm = nc.tensor.matmul(out_bank("g")[q:q + FFN_M, :], w2_diag[:, j], hidden[:, j],
                                          start=j < 2, stop=j >= PAIRS_J - 2)
                mm.then_inc(pe_out, 1)
                pe.wait_ge(act_freed, act_count("g", k))
                for o in range(2):
                    bank_free(f"ffn{o}", k)
                    for j in range(2):
                        t = 2 * o + j
                        mm = nc.tensor.matmul(out_bank(f"ffn{o}")[:, j * DIM:(j + 1) * DIM],
                                              gT[:, t * P:(t + 1) * P], wout[:, :], start=True, stop=True)
                    mm.then_inc(pe_out, 1)

            with pe.Fori(0, BESIDE // 2) as m:
                for u in range(2):
                    block_of(2 * m + u, m, u)
            for k in range(BESIDE, CHUNKS):
                block_of(k, k // 2, k % 2)
            pe.wait_ge(max_kept, CHUNKS)
            nc.tensor.matmul(bank[0][0:1, 0:P], norm_max[:, 0:1], ident[:, :], start=True, stop=True)\
                .then_inc(setup_pe, 1)


def phase_two(nc, select, q_parts, k_parts, values, index_qk, residual, out_rows,
              ident, ident_b, exclude_diag, woT, flag):
    f32, bf16, f8 = mybir.dt.float32, mybir.dt.bfloat16, mybir.dt.float8e4
    ALU, ACT, AX = mybir.AluOpType, mybir.ActivationFunctionType, mybir.AxisListType

    with ExitStack() as ctx:
        def sb(name, shape, dt=f32):
            return ctx.enter_context(nc.sbuf_tensor(name, shape, dt))

        def sem(name):
            return ctx.enter_context(nc.semaphore(name))

        keys = sb("keys", [P, HEADS, SEQ], bf16)
        queries = [select.first_queries, sb("queries1", [P, HEADS, CHUNK], bf16)]
        v_sb = sb("v_sb", [P, QUADS, KEY_TILES, 4 * V_COLS])
        window_keys = select.window_keys
        masks = [select.first_masks, sb("masks1", [P, ASSOC_TILES, CHUNK], f8)]
        probs = [sb(f"probs{p}", [P, 4, CHUNK]) for p in range(2)]
        heads_out = sb("heads_out", [P, QUADS, CHUNK])
        inverse = sb("inverse", [P, TILES * 4])
        normed = sb("normed", [P, TILES, DIM])
        normedT = sb("normedT", [P, CC, CHUNK])
        y = sb("y", [P, TILES, DIM])
        maxima = sb("maxima", [P, TILES, HEADS])
        shift_rest = sb("shift_rest", [HEADS, CHUNK])
        shift_parts = sb("shift_parts", [HEADS, SHIFT_ROWS, CHUNK], bf16)
        scores = ctx.enter_context(nc.psum_tensor("scores", [P, 6 * CHUNK], f32))
        outs = ctx.enter_context(nc.psum_tensor("outs", [P, CHUNK], f32))
        misc = select.misc

        tables_ready, ones_ready, passed = sem("tables_ready"), sem("ones_ready"), sem("passed")
        keys_loaded = [sem(f"keys_loaded{q}") for q in range(QUADS)]
        q_loaded = [select.q_loaded, sem("q_loaded1")]
        shift_loaded = [sem(f"shift_loaded{u}") for u in range(2)]
        window_loaded, res_loaded = select.window_loaded, sem("res_loaded")
        scored, exps_done, probs_used = sem("scored"), sem("exps_done"), sem("probs_used")
        outs_saved = sem("outs_saved")
        misc_filled, misc_drained = select.misc_filled, select.misc_drained
        inverse_ready, split_step, shift_split = sem("inverse_ready"), sem("split_step"), sem("shift_split")
        y_stored = sem("y_stored")
        all_scored, all_reduced, all_turned = sem("all_scored"), sem("all_reduced"), sem("all_turned")
        all_step, all_read, all_split, all_loaded = sem("all_step"), sem("all_read"), sem("all_split"), sem("all_loaded")
        block = ctx.enter_context(nc.Block())

        SCORE_BUFS, PROB_BUFS, SAVED = 3, 2, QUADS

        def jobs_before(n):
            return PRO_JOBS + n * NJOBS

        def quad_used(n, q):
            return PROB_BUFS + STEPS * n + KEY_TILES * (q + 1)

        @block.sync
        def _(sp):
            def load_shift(u, loaded):
                for j in range(SHIFT_ROWS):
                    sp.dma_start(queries[u][STACK + j:STACK + j + 1, :, :], shift_parts[:, j]).then_inc(loaded, 16)

            sp.wait_ge(shift_split, 1)
            load_shift(0, shift_loaded[0])
            use_all = sp.value_load(flag[0:1, 0:1], min_val=0, max_val=1)
            with sp.Fori(0, CHUNKS // 2) as m:
                for u in range(2):
                    n = 2 * m + u
                    with sp.If(use_all != 0):
                        sp.wait_ge(shift_loaded[u], 16 * SHIFT_ROWS * (m + 1))
                        sp.wait_ge(all_split, n + 1)
                        load_shift(u, all_loaded)
                    sp.wait_ge(y_stored, 16 * (n + 1))
                    sp.dma_start(y[:, :, :], residual[bass.ds(((n + CHUNKS - 1) % CHUNKS) * CHUNK, CHUNK)]
                                 .rearrange("(t p) d -> p t d", p=P)).then_inc(res_loaded, 16)
                    sp.wait_ge(probs_used, quad_used(n, -1))
                    select.load_queries(sp, q_parts, queries[1 - u], q_loaded[1 - u], (n + 1) % CHUNKS)
                    for t in range(TILES):
                        if t == 0:
                            sp.wait_ge(misc_filled, jobs_before(n))
                        else:
                            sp.wait_ge(misc_filled, jobs_before(n) + job_position("index", (t - 1, 3)) + 1)
                        select.load_index_q(sp, (TILES * n + t + INDEX_LEAD + 1) % (TOKENS // P), (t + 1) % 2)
                        if t == 0:
                            sp.wait_ge(misc_drained, jobs_before(n) + job_position("proj", 1) + 1)
                            stand(sp, passed)
                            with sp.If(n > 0):
                                sp.dma_start(out_rows[bass.ds(((n + CHUNKS - 1) % CHUNKS) * CHUNK, CHUNK)]
                                             .rearrange("(t p) d -> p t d", p=P), y[:, :, :]).then_inc(y_stored, 16)
                    sp.wait_ge(shift_split, n + 2)
                    load_shift(1 - u, shift_loaded[1 - u])
            sp.wait_ge(y_stored, 16 * (CHUNKS + 1))
            last_rows = slice((CHUNKS - 1) * CHUNK, CHUNKS * CHUNK)
            sp.dma_start(y[:, :, :], residual[last_rows].rearrange("(t p) d -> p t d", p=P)).then_inc(res_loaded, 16)
            sp.wait_ge(misc_drained, jobs_before(CHUNKS) + QUADS + CC + 2)
            sp.dma_start(out_rows[last_rows].rearrange("(t p) d -> p t d", p=P), y[:, :, :]).then_inc(y_stored, 16)
            sp.wait_ge(y_stored, 16 * (CHUNKS + 2))
            for u in range(2):
                sp.wait_ge(q_loaded[u], 16 * len(PAIRS) * (CHUNKS // 2 + (u == 0)))
                sp.wait_ge(shift_loaded[u], 16 * SHIFT_ROWS * (CHUNKS // 2 + (u == 0)))
            sp.wait_ge(select.index_q_loaded[0], 16 * (TOKENS // P // 2 + 4))
            sp.wait_ge(select.index_q_loaded[1], 16 * (TOKENS // P // 2 + 3))

        @block.gpsimd
        def _(pool):
            def load_quad(b, q):
                heads = slice(4 * q, 4 * q + 4)
                for dst, src in stacked(keys[:, heads], k_parts, 1, heads, bass.ds(b * SEQ, SEQ)):
                    pool.dma_start(dst, src).then_inc(keys_loaded[q], 16)
                pool.dma_start(v_sb[:, q], values[bass.ds(b * SEQ, SEQ), q * 4 * V_COLS:(q + 1) * 4 * V_COLS]
                               .rearrange("(t p) c -> p t c", p=P)).then_inc(keys_loaded[q], 16)

            for q in range(QUADS):
                nc.gpsimd.memset(keys[STACK:ROWS, 4 * q:4 * q + 4].rearrange("p h t -> p (h t)").bitcast(f32),
                                 BF16_ONES).then_inc(ones_ready, 1)
                load_quad(0, q)
            with pool.Fori(1, BATCH) as b:
                before = jobs_before(b * (CHUNKS // BATCH) - 2)
                pool.wait_ge(misc_filled, before + job_position("index", (1, 3)) + 1)
                select.load_index_k(pool, b)
                pool.wait_ge(misc_filled, before + job_position("window", (TILES - 1, QUADS - 1)) + 1)
                select.load_window_keys(pool, k_parts, b)
                for q in range(QUADS):
                    pool.wait_ge(probs_used, quad_used(b * (CHUNKS // BATCH) - 1, q))
                    load_quad(b, q)
            before = jobs_before(CHUNKS - 2)
            pool.wait_ge(misc_filled, before + job_position("index", (1, 3)) + 1)
            select.load_index_k(pool, 0)
            pool.wait_ge(misc_filled, before + job_position("window", (TILES - 1, QUADS - 1)) + 1)
            select.load_window_keys(pool, k_parts, 0)
            pool.wait_ge(select.index_k_loaded, 16 * (BATCH + 1))
            pool.wait_ge(window_loaded, 16 * len(PAIRS) * (BATCH + 1))

        @block.scalar
        def _(act):
            def save_outs(n, q):
                act.wait_ge(probs_used, quad_used(n, q))
                act.wait_ge(misc_filled, jobs_before(n) + job_position("norm", q) + 1)
                nc.scalar.activation(heads_out[:, q], outs[:, :], ACT.Copy).then_inc(outs_saved, 1)

            act.wait_ge(tables_ready, 1)
            act.sem_inc(exps_done, SCORE_BUFS)
            act.sem_inc(outs_saved, SAVED)
            with act.Fori(0, CHUNKS // 2) as m:
                for u in range(2):
                    n = 2 * m + u
                    for s in range(STEPS):
                        for h in range(2):
                            act.wait_ge(scored, 2 * STEPS * n + 2 * s + h + 1)
                            if h == 0:
                                act.wait_ge(probs_used, STEPS * n + s + 1)
                            buf = (2 * s + h) % SCORE_BUFS
                            nc.scalar.activation(probs[s % 2][:, 2 * h:2 * h + 2],
                                                 scores[:, buf * 2 * CHUNK:(buf + 1) * 2 * CHUNK]
                                                 .rearrange("p (a s) -> p a s", a=2), ACT.Exp).then_inc(exps_done, 1)
                        if s % KEY_TILES == 0 and s > 0:
                            save_outs(n, s // KEY_TILES - 1)
                        if s in JOBS:
                            pos, kind, arg = JOBS[s]
                            if kind == "index":
                                t, i = arg
                                select.drain_index(act, jobs_before(n) + pos, TILES * n + t + INDEX_LEAD, t % 2, i)
                            elif kind == "mask":
                                select.drain_mask(act, passed, jobs_before(n) + pos, masks[1 - u], *arg)
                    save_outs(n, QUADS - 1)

        @block.vector
        def _(dve):
            def drain_window(count, t, q):
                dve.wait_ge(misc_filled, count + 1)
                nc.vector.reduce_max(maxima[:, t, 4 * q:4 * q + 4], misc[:, :].rearrange("p (h w) -> p h w", h=4), AX.X)\
                    .then_inc(misc_drained, 1)

            def split_shift(step, before, read, read_before, done):
                nc.vector.tensor_scalar(shift_parts[:, 0], misc[0:HEADS, :], -1.0, None, ALU.mult).then_inc(step, 1)
                dve.wait_ge(step, before + 1)
                nc.vector.scalar_tensor_tensor(shift_rest[:, :], misc[0:HEADS, :], -1.0, shift_parts[:, 0],
                                               ALU.mult, ALU.subtract).then_inc(read, 1)
                dve.wait_ge(read, read_before + 1)
                nc.vector.tensor_copy(shift_parts[:, 1], shift_rest[:, :]).then_inc(step, 1)
                dve.wait_ge(step, before + 2)
                nc.vector.tensor_tensor(shift_parts[:, 2], shift_rest[:, :], shift_parts[:, 1], ALU.subtract)\
                    .then_inc(done, 1)

            def drain_norm(count, done, q):
                dve.wait_ge(misc_filled, count + 1)
                blocks = misc[:, :].rearrange("p (b c) -> p b c", c=32)
                nc.vector.reciprocal(inverse[:, :], blocks[:, :, HEAD_DIM]).then_inc(inverse_ready, 1)
                dve.wait_ge(inverse_ready, done + 1)
                nc.vector.tensor_tensor(
                    normed[:, :, 4 * q * HEAD_DIM:4 * (q + 1) * HEAD_DIM].rearrange("p t (h i) -> p t h i", h=4),
                    misc[:, :].rearrange("p (t h c) -> p t h c", t=TILES, h=4)[:, :, :, 0:HEAD_DIM],
                    inverse[:, :].rearrange("p (t h) -> p t h", h=4).unsqueeze(3)
                    .to_broadcast([P, TILES, 4, HEAD_DIM]), ALU.mult).then_inc(misc_drained, 1)

            def drain_turn(count, c):
                dve.wait_ge(misc_filled, count + 1)
                nc.vector.tensor_copy(normedT[:, c], misc[:, :]).then_inc(misc_drained, 1)

            def drain_proj(count, n, c):
                dve.wait_ge(misc_filled, count + 1)
                dve.wait_ge(res_loaded, 16 * (n + 1))
                part = y[:, 2 * c:2 * c + 2]
                nc.vector.tensor_tensor(part, misc[:, :].rearrange("p (t d) -> p t d", t=2), part, ALU.add)\
                    .then_inc(misc_drained, 1)

            nc.vector.memset(outs[:, :], 0.0).then_inc(tables_ready, 1)
            dve.wait_ge(tables_ready, 1)
            nc.vector.memset(heads_out[:, :, :], 1.0).then_inc(tables_ready, 1)
            dve.wait_ge(tables_ready, 2)
            dve.sem_inc(y_stored, 32)
            dve.sem_inc(probs_used, PROB_BUFS)
            dve.sem_inc(all_reduced, 1)
            for t in range(TILES):
                for q in range(QUADS):
                    drain_window(pro_job("window", t, q), t, q)
            dve.wait_ge(misc_filled, pro_job("shift", 0) + 1)
            split_shift(split_step, 0, misc_drained, pro_job("shift", 0), shift_split)
            use_all = dve.value_load(flag[0:1, 0:1], min_val=0, max_val=1)
            with dve.Fori(0, CHUNKS // 2) as m:
                for u in range(2):
                    n = 2 * m + u
                    with dve.If(use_all != 0):
                        with dve.Fori(0, HEADS) as h:
                            for t in range(TILES):
                                dve.wait_ge(all_scored, TILES * HEADS * n + TILES * h + t + 1)
                                stand(dve, passed)
                                nc.vector.reduce_max(maxima[:, t, bass.ds(h, 1)], scores[:, 0:SEQ], AX.X)\
                                    .then_inc(all_reduced, 1)
                        dve.wait_ge(all_turned, n + 1)
                        dve.wait_ge(shift_loaded[u], 16 * SHIFT_ROWS * (m + 1))
                        split_shift(all_step, 2 * n, all_read, n, all_split)
                        dve.wait_ge(all_loaded, 16 * SHIFT_ROWS * (n + 1))
                        stand(dve, passed)
                    for s in range(STEPS):
                        t, r = divmod(s, WINDOW_STEPS)
                        if s in JOBS:
                            pos, kind, arg = JOBS[s]
                            count = jobs_before(n) + pos
                            if kind == "norm":
                                drain_norm(count, QUADS * n + arg, arg)
                            elif kind == "turn":
                                drain_turn(count, arg)
                            elif kind == "proj":
                                drain_proj(count, n, arg)
                            elif kind == "window":
                                drain_window(count, *arg)
                            elif kind == "shift":
                                dve.wait_ge(shift_loaded[u], 16 * SHIFT_ROWS * (m + 1))
                                dve.wait_ge(misc_filled, count + 1)
                                split_shift(split_step, 2 * (n + 1), misc_drained, count, shift_split)
                        tile, p = TILES * n + t + TOPK_LEAD, (t + TOPK_LEAD) % 2
                        select.topk_op(dve, passed, tile, p, r, jobs_before(n) + (0 if t == 0 else job_position("index", (t - 1, 3)) + 1))
                        if r == WINDOW_STEPS - 1:
                            dve.wait_ge(misc_filled, jobs_before(n) + job_position("mask", (t, 1)) + 1)
                            select.topk_op(dve, passed, tile, p, r + 1)
            last = jobs_before(CHUNKS)
            for q in range(QUADS):
                drain_norm(last + q, QUADS * CHUNKS + q, q)
            for c in range(CC):
                drain_turn(last + QUADS + c, c)
            for c in range(2):
                drain_proj(last + QUADS + CC + c, CHUNKS, c)

        @block.tensor
        def _(pe):
            def fill_window(count, u, t, q):
                pe.wait_ge(misc_drained, count)
                for j in range(4):
                    mm = nc.tensor.matmul(misc[:, j * WINDOW:(j + 1) * WINDOW],
                                          queries[u][0:STACK, 4 * q + j, t * P:(t + 1) * P],
                                          window_keys[0:STACK, 4 * q + j, :], start=True, stop=True)
                mm.then_inc(misc_filled, 1)

            def turn_maxima(signal):
                for t in range(TILES):
                    mm = nc.tensor.matmul(misc[0:HEADS, t * P:(t + 1) * P], maxima[:, t], ident[:, :],
                                          start=True, stop=True)
                mm.then_inc(signal, 1)

            def fill_norm(count, n, q):
                pe.wait_ge(misc_drained, count)
                pe.wait_ge(outs_saved, QUADS * n + q + 1)
                for t in range(TILES):
                    tr = nc.tensor.transpose(misc[:, t * P:(t + 1) * P], heads_out[:, q, t * P:(t + 1) * P], ident[:, :])
                tr.then_inc(misc_filled, 1)

            def fill_turn(count, c):
                pe.wait_ge(misc_drained, count)
                for t in range(TILES):
                    tr = nc.tensor.transpose(misc[:, t * P:(t + 1) * P], normed[:, t, c * P:(c + 1) * P], ident[:, :])
                tr.then_inc(misc_filled, 1)

            def fill_proj(count, half):
                pe.wait_ge(misc_drained, count)
                for j in range(2):
                    t = 2 * half + j
                    for c in range(CC):
                        mm = nc.tensor.matmul(misc[:, j * DIM:(j + 1) * DIM], normedT[:, c, t * P:(t + 1) * P],
                                              woT[:, c], start=c == 0, stop=c == CC - 1)
                mm.then_inc(misc_filled, 1)

            def weigh_values(n, s):
                q, kt = divmod(s, KEY_TILES)
                pe.wait_ge(exps_done, SCORE_BUFS + 2 * STEPS * n + 2 * s + 2)
                if kt == 0:
                    pe.wait_ge(outs_saved, SAVED + QUADS * n + q)
                for j in range(4):
                    mm = nc.tensor.matmul(outs[32 * j:32 * j + V_COLS, :], v_sb[:, q, kt, j * V_COLS:(j + 1) * V_COLS],
                                          probs[s % 2][:, j], start=kt == 0, stop=kt == KEY_TILES - 1)
                mm.then_inc(probs_used, 1)

            pe.wait_ge(tables_ready, 2)
            pe.wait_ge(window_loaded, 16 * len(PAIRS))
            pe.wait_ge(q_loaded[0], 16 * len(PAIRS))
            for t in range(TILES):
                for q in range(QUADS):
                    fill_window(pro_job("window", t, q), 0, t, q)
            pe.wait_ge(misc_drained, pro_job("shift", 0))
            turn_maxima(misc_filled)
            use_all = pe.value_load(flag[0:1, 0:1], min_val=0, max_val=1)
            with pe.Fori(0, CHUNKS // 2) as m:
                for u in range(2):
                    n = 2 * m + u
                    pe.wait_ge(misc_drained, jobs_before(n))
                    pe.wait_ge(shift_loaded[u], 16 * SHIFT_ROWS * (m + 1))
                    with pe.If(use_all != 0):
                        for q in range(QUADS):
                            pe.wait_ge(keys_loaded[q], 16 * (len(PAIRS) + 1) * (n // (CHUNKS // BATCH) + 1))
                        pe.wait_ge(exps_done, SCORE_BUFS + 2 * STEPS * n)
                        stand(pe, passed)
                        with pe.Fori(0, HEADS) as h:
                            for t in range(TILES):
                                pe.wait_ge(all_reduced, TILES * HEADS * n + TILES * h + t + 1)
                                for c in range(SEQ // CHUNK):
                                    nc.tensor.matmul(scores[:, c * CHUNK:(c + 1) * CHUNK],
                                                     queries[u][0:STACK, bass.ds(h, 1), t * P:(t + 1) * P],
                                                     keys[0:STACK, bass.ds(h, 1), c * CHUNK:(c + 1) * CHUNK],
                                                     start=True, stop=False)
                                    blocks = range(4 * c, min(4 * c + 4, ASSOC_TILES))
                                    for a in blocks:
                                        mm = nc.tensor.matmul(scores[:, a * P:(a + 1) * P],
                                                              masks[u][:, a, t * P:(t + 1) * P], exclude_diag[:, :],
                                                              start=False, stop=a == blocks[-1])
                                mm.then_inc(all_scored, 1)
                        pe.wait_ge(all_reduced, TILES * HEADS * (n + 1) + 1)
                        turn_maxima(all_turned)
                        pe.wait_ge(all_loaded, 16 * SHIFT_ROWS * (n + 1))
                        stand(pe, passed)
                    for s in range(STEPS):
                        q, kt = divmod(s, KEY_TILES)
                        if kt == 0:
                            pe.wait_ge(ones_ready, q + 1)
                            pe.wait_ge(keys_loaded[q], 16 * (len(PAIRS) + 1) * (n // (CHUNKS // BATCH) + 1))
                        for half in range(2):
                            i = 2 * s + half
                            buf = i % SCORE_BUFS
                            used = i - SCORE_BUFS if i >= SCORE_BUFS else (2 * STEPS - 1 - (2 * STEPS - 1 - i) % SCORE_BUFS) - 2 * STEPS
                            pe.wait_ge(exps_done, SCORE_BUFS + 2 * STEPS * n + used + 1)
                            for j in range(2):
                                head = 4 * q + 2 * half + j
                                bank = scores[:, (2 * buf + j) * CHUNK:(2 * buf + j + 1) * CHUNK]
                                mm = nc.tensor.matmul(bank, keys[0:ROWS, head, kt * P:(kt + 1) * P],
                                                      queries[u][0:ROWS, head, :], start=True, stop=kt >= ASSOC_TILES)
                                if kt < ASSOC_TILES:
                                    mm = nc.tensor.matmul(bank, exclude_diag[:, :], masks[u][:, kt, :],
                                                          start=False, stop=True)
                            mm.then_inc(scored, 1)
                        if s in JOBS:
                            pos, kind, arg = JOBS[s]
                            count = jobs_before(n) + pos
                            if kind == "index":
                                t, i = arg
                                loads = (n + 1 + (t >= 2)) // (CHUNKS // BATCH) + 1
                                select.fill_index(pe, count, TILES * n + t + INDEX_LEAD, t % 2, i, loads)
                            elif kind == "mask":
                                select.fill_mask(pe, count, TILES * n + arg[0] + MASK_LEAD, arg[1])
                            elif kind == "window":
                                if arg == (0, 0):
                                    pe.wait_ge(q_loaded[1 - u], 16 * len(PAIRS) * (m + u + 1))
                                    pe.wait_ge(window_loaded, 16 * len(PAIRS) * ((n + 1) // (CHUNKS // BATCH) + 1))
                                fill_window(count, 1 - u, *arg)
                            elif kind == "shift":
                                pe.wait_ge(misc_drained, count)
                                turn_maxima(misc_filled)
                            elif kind == "norm":
                                fill_norm(count, n, arg)
                            elif kind == "turn":
                                fill_turn(count, arg)
                            else:
                                fill_proj(count, arg)
                        if s > 0:
                            weigh_values(n, s - 1)
                    weigh_values(n, STEPS - 1)
            last = jobs_before(CHUNKS)
            for q in range(QUADS):
                fill_norm(last + q, CHUNKS, q)
            for c in range(CC):
                fill_turn(last + QUADS + c, c)
            for half in range(2):
                fill_proj(last + QUADS + CC + half, half)


_INS = ['L0_attn_x', 'L0_attn_wq', 'L0_attn_bq', 'L0_attn_wk', 'L0_attn_bk', 'L0_attn_wv', 'L0_attn_bv', 'L0_attn_wo',
        'L0_attn_bo', 'L0_attn_wqi', 'L0_attn_bqi', 'L0_attn_wki', 'L0_attn_bki', 'L0_ffn_Win', 'L0_ffn_bin_',
        'L0_ffn_W1', 'L0_ffn_b1', 'L0_ffn_W2', 'L0_ffn_b2', 'L0_ffn_Wout', 'L0_ffn_bout']
_OUTS = [((BATCH, SEQ, DIM), 'float32')]


def kernel(**inputs):
    import numpy as _np
    import concourse.bacc as _bacc
    from concourse import mybir as _mybir
    from concourse.bass_utils import run_bass_kernel_spmd as _run

    nc = _bacc.Bacc("TRN2", target_bir_lowering=False, num_devices=1)
    arrays, args = {}, []
    for name in _INS:
        a = _np.ascontiguousarray(inputs[name])
        arrays[f"in_{name}_dram"] = a
        args.append(nc.dram_tensor(f"in_{name}_dram", a.shape, _mybir.dt.from_np(a.dtype), kind="ExternalInput").ap())
    for i, (shape, dtype) in enumerate(_OUTS):
        dt = _mybir.dt.from_np(_np.dtype(dtype))
        args.append(nc.dram_tensor(f"out_{i}_dram", shape, dt, kind="ExternalOutput").ap())
    build(nc, *args)
    r = _run(nc, [arrays], core_ids=[0])
    got = tuple(r.results[0][f"out_{i}_dram"] for i in range(len(_OUTS)))
    return got[0]
```
